# Optimizing a Trainium2 kernel written in Bass

```python
import numpy as np
import jax
import jax.numpy as jnp

def _softmax(x, axis=-1):
    return jax.nn.softmax(x, axis=axis)

def _gelu(x):
    return jax.nn.gelu(x, approximate=True)

def _silu(x):
    return jax.nn.silu(x)

def _sigmoid(x):
    return jax.nn.sigmoid(x)

def _layernorm(x, axis=-1, eps=1e-05):
    m = jnp.mean(x, axis=axis, keepdims=True)
    v = jnp.var(x, axis=axis, keepdims=True)
    return (x - m) / jnp.sqrt(v + eps)

def _scatter_add(tgt, idx, src, axis=0):
    return tgt.at[idx].add(src)

def _segment_sum(src, seg, n):
    return jax.ops.segment_sum(src, seg, n)
kernel_name = 'mk_adj_ffn_d1_adj_r2_d8fef7'

def setup_inputs(seed: int=0):
    np.random.seed(seed)
    _w = jnp.asarray

    def _rec_inputs():
        import jax
        import jax.numpy as jnp
        _gk = jax.random.key(seed)
        x = 7.22e-05 + 1 * jax.random.normal(jax.random.fold_in(_gk, 1), (128, 64, 256), jnp.float32)
        _a = jax.random.bernoulli(jax.random.fold_in(_gk, 2), 0.0625, (128, 64, 64))
        adj = _a.astype(jnp.int32)
        return (x, adj)
    x, adj = _rec_inputs()

    def _L0_gnn_setup():
        import jax, jax.numpy as jnp
        import numpy as np
        ALPHA = 0.2
        MASK_VAL = -1000000000.0
        key = jax.random.key(seed)
        k1, k2, k3, k4 = jax.random.split(key, 4)
        B, N, F_in, F_out = (8, 1024, 256, 256)
        h = jax.random.normal(k1, (B, N, F_in), dtype=jnp.float32)
        adj = jax.random.randint(k2, (B, N, N), 0, 2, dtype=jnp.int32)

        def xavier(k, shape, gain=1.414):
            fan_in, fan_out = (shape[0], shape[1])
            bound = gain * np.sqrt(6.0 / (fan_in + fan_out))
            return jax.random.uniform(k, shape, jnp.float32, -bound, bound)
        W = xavier(k3, (F_in, F_out))
        a = xavier(k4, (2 * F_out, 1))
        return {'h': h, 'adj': adj, 'W': W, 'a': a}
    _L0_gnn_all = _L0_gnn_setup()
    _L0_gnn_in = {k: v for k, v in _L0_gnn_all.items() if k in ('W', 'a')}
    del _L0_gnn_all

    def _L0_ffn_setup():
        import jax, jax.numpy as jnp
        import numpy as np
        B, S, D = (2, 1024, 256)
        E, H, TOP_K = (8, 512, 2)
        SCALE = 1.0
        key = jax.random.key(seed)
        ks = jax.random.split(key, 7)
        s = lambda fan_in: 1.0 / np.sqrt(fan_in)
        return {'x': jax.random.normal(ks[0], (B, S, D), dtype=jnp.float32), 'gate_w': jax.random.normal(ks[1], (E, D), dtype=jnp.float32) * s(D), 'w1': jax.random.normal(ks[2], (E, H, D), dtype=jnp.float32) * s(D), 'w2': jax.random.normal(ks[3], (E, D, H), dtype=jnp.float32) * s(H), 'sg_gate': jax.random.normal(ks[4], (H, D), dtype=jnp.float32) * s(D), 'sg_up': jax.random.normal(ks[5], (H, D), dtype=jnp.float32) * s(D), 'sg_down': jax.random.normal(ks[6], (D, H), dtype=jnp.float32) * s(H)}
    _L0_ffn_all = _L0_ffn_setup()
    _L0_ffn_in = {k: v for k, v in _L0_ffn_all.items() if k in ('gate_w', 'w1', 'w2', 'sg_gate', 'sg_up', 'sg_down')}
    del _L0_ffn_all
    return {'x': x, 'adj': adj, 'L0_gnn_W': _L0_gnn_in['W'], 'L0_gnn_a': _L0_gnn_in['a'], 'L0_ffn_gate_w': _L0_ffn_in['gate_w'], 'L0_ffn_w1': _L0_ffn_in['w1'], 'L0_ffn_w2': _L0_ffn_in['w2'], 'L0_ffn_sg_gate': _L0_ffn_in['sg_gate'], 'L0_ffn_sg_up': _L0_ffn_in['sg_up'], 'L0_ffn_sg_down': _L0_ffn_in['sg_down']}

def reference(x, adj, L0_gnn_W, L0_gnn_a, L0_ffn_gate_w, L0_ffn_w1, L0_ffn_w2, L0_ffn_sg_gate, L0_ffn_sg_up, L0_ffn_sg_down):
    import jax
    import jax.numpy as jnp

    def _L0_gnn_ref(h, adj, W, a):
        import jax, jax.numpy as jnp
        import numpy as np
        ALPHA = 0.2
        MASK_VAL = -1000000000.0
        Fout = W.shape[1]
        Wh = jnp.matmul(h, W)
        a1 = a[:Fout, 0]
        a2 = a[Fout:, 0]
        e_i = jnp.einsum('bnf,f->bn', Wh, a1)
        e_j = jnp.einsum('bnf,f->bn', Wh, a2)
        e = e_i[:, :, None] + e_j[:, None, :]
        e = jax.nn.leaky_relu(e, negative_slope=ALPHA)
        e = jnp.where(adj == 0, MASK_VAL, e)
        attention = jax.nn.softmax(e, axis=2)
        h_prime = jnp.matmul(attention, Wh)
        return jax.nn.elu(h_prime)

    def _L0_ffn_ref(x, gate_w, w1, w2, sg_gate, sg_up, sg_down):
        import jax, jax.numpy as jnp
        import numpy as np
        B, S, D = (2, 1024, 256)
        E, H, TOP_K = (8, 512, 2)
        SCALE = 1.0
        b, s_len, d = x.shape
        xf = x.reshape(-1, d)
        n = xf.shape[0]
        logits = xf @ gate_w.T * SCALE
        topk_w, idx = jax.lax.top_k(logits, TOP_K)
        topk_w = jax.nn.softmax(topk_w, axis=-1)
        comb = jnp.zeros((n, E), dtype=xf.dtype).at[jnp.arange(n)[:, None], idx].add(topk_w)
        h = jax.nn.silu(jnp.einsum('td,ehd->teh', xf, w1))
        eo = jnp.einsum('teh,edh->ted', h, w2)
        routed = jnp.einsum('te,ted->td', comb, eo)
        shared = jax.nn.silu(xf @ sg_gate.T) * (xf @ sg_up.T) @ sg_down.T
        return (routed + shared).reshape(b, s_len, d)
    x = x + _L0_gnn_ref(_layernorm(x, axis=-1), adj, L0_gnn_W, L0_gnn_a)
    x = x + _L0_ffn_ref(_layernorm(x, axis=-1), L0_ffn_gate_w, L0_ffn_w1, L0_ffn_w2, L0_ffn_sg_gate, L0_ffn_sg_up, L0_ffn_sg_down)
    return x

_drawn_inputs = setup_inputs


def setup_inputs(seed=0):
    import zlib

    import numpy as np

    out = dict(_drawn_inputs(seed))
    spreads = {}
    factors = {}
    for name, (base, spread) in spreads.items():
        noise = np.random.default_rng([zlib.crc32(name.encode()), seed]).standard_normal(out[name].shape)
        drawn = base * np.exp(spread * noise) if base else spread * noise
        out[name] = jnp.asarray(drawn.astype(out[name].dtype))
    for name, factor in factors.items():
        out[name] = (out[name] * factor).astype(out[name].dtype)
    return out
```

```python
from contextlib import ExitStack

import concourse.bass as bass
from concourse import mybir

ALU = mybir.AluOpType
ACT = mybir.ActivationFunctionType
AX = mybir.AxisListType
F32 = mybir.dt.float32
F32R = mybir.dt.float32r
BF16 = mybir.dt.bfloat16
I32 = mybir.dt.int32
U32 = mybir.dt.uint32

P = 128
EPS = 1e-5
SLOPE = 0.2
MASK = -1e30


def inside(n, count):
    return not isinstance(n, int) or 0 <= n < count


def through(g, par, each):
    return (g + (2 - par)) * each


def hold(eng, sem):
    eng.sem_inc(sem, 1)


class Chain:

    def __init__(self, eng, sem, done):
        self.eng, self.sem, self.value = eng, sem, done

    def step(self, ins):
        ins.then_inc(self.sem, 1)
        self.value = self.value + 1

    def wait(self):
        self.eng.wait_ge(self.sem, self.value)


def wait_if(eng, sem, value):
    if not isinstance(value, int) or value > 0:
        eng.wait_ge(sem, value)


def gat_moe(nc, x, adj, W, a, gate_wT, experts, shared, out):
    T, D = x.shape
    N = adj.shape[1]
    E = gate_wT.shape[2]
    KD = D // P
    GT = 4
    TG = GT * P
    NG = T // TG
    H = 512
    KH = H // P
    WC = KD * H
    REG = T + P
    NB = 2 * T // P + E
    RANKS = E * E
    ST_L, ST_OH, ST_POS, ST = 0, GT * E, 3 * GT * E, 3 * GT * E + 2 * GT

    regions = nc.dram_tensor("regions", [E * REG, D], F32, kind="Internal").ap()
    x2_dram = nc.dram_tensor("x2_rows", [T, D], F32, kind="Internal").ap()
    xT_dram = nc.dram_tensor("xn2_cols", [P, NG, KD, TG], F32, kind="Internal").ap()
    y_dram = nc.dram_tensor("expert_rows", [NB * P, D], F32, kind="Internal").ap()

    with ExitStack() as top:
        def sem(name):
            return top.enter_context(nc.semaphore(name))

        def keep(name, shape, dt=F32):
            return top.enter_context(nc.sbuf_tensor(name, shape, dt))

        ident = keep("ident", [P, P])
        stash_all = keep("stash_all", [P, NG, ST])
        tile_row = keep("tile_row", [P, NB], I32)
        tile_exp = keep("tile_exp", [P, NB], I32)
        row_of = keep("row_of", [P, NG, 2 * GT], U32)
        weight_of = keep("weight_of", [P, NG, 2 * GT])

        part_a(nc, top, sem, locals())
        part_b(nc, top, sem, locals())
        part_c(nc, top, sem, locals())


def part_a(nc, top, sem, v):
    x, adj, W, a, gate_wT = v["x"], v["adj"], v["W"], v["a"], v["gate_wT"]
    T, D, N, E, KD, GT, TG, NG = (v[k] for k in ("T", "D", "N", "E", "KD", "GT", "TG", "NG"))
    REG, NB, RANKS = v["REG"], v["NB"], v["RANKS"]
    ST_L, ST_OH, ST_POS, ST = v["ST_L"], v["ST_OH"], v["ST_POS"], v["ST"]
    ident, stash_all, tile_row, tile_exp = v["ident"], v["stash_all"], v["tile_row"], v["tile_exp"]
    row_of, weight_of = v["row_of"], v["weight_of"]
    regions, x2_dram, xT_dram = v["regions"], v["x2_dram"], v["xT_dram"]
    WX = D + 2

    with ExitStack() as ctx:
        def sb(name, shape, dt=F32):
            return ctx.enter_context(nc.sbuf_tensor(name, shape, dt))

        def psum(name, shape):
            return ctx.enter_context(nc.psum_tensor(name, shape, F32))

        same_graph = sb("same_graph", [P, P])
        node_of = sb("node_of", [P, N])
        before_f = sb("before_f", [P, P])
        before = sb("before", [P, P], BF16)
        ones_b = sb("ones_b", [P, P], BF16)
        lower_e = sb("lower_e", [P, E, E])
        exp_base_i = sb("exp_base_i", [P, E], I32)
        exp_base = sb("exp_base", [P, E])
        half = sb("half", [P, GT])
        lane_i = sb("lane_i", [P, 1], I32)
        lane = sb("lane", [P, 1])
        jrow_i = sb("jrow_i", [P, NB], I32)
        jrow = sb("jrow", [P, NB])
        jrow128 = sb("jrow128", [P, NB])
        zero_rows = sb("zero_rows", [P, D])
        w_ext = sb("w_ext", [P, KD, WX])
        a_rows = sb("a_rows", [P, 2, D])
        wa_tmp = sb("wa_tmp", [P, D])
        gw = sb("gw", [P, KD, E])
        x_sb = sb("x_sb", [P, 2, GT, D])
        adj_sb = sb("adj_sb", [P, 2, GT, N], I32)
        stats1 = sb("stats1", [P, GT, 6])
        stats2 = sb("stats2", [P, GT, 6])
        mv1 = sb("mv1", [P, 2, GT, 2])
        mv2 = sb("mv2", [P, 2, GT, 2])
        var_eps1 = sb("var_eps1", [P, GT])
        var_eps2 = sb("var_eps2", [P, GT])
        rstd1 = sb("rstd1", [P, 2, GT])
        rstd2 = sb("rstd2", [P, 2, GT])
        shift1 = sb("shift1", [P, 2, GT])
        shift2 = sb("shift2", [P, 2, GT])
        prod1 = sb("prod1", [P, GT])
        prod2 = sb("prod2", [P, GT])
        xn = sb("xn", [P, GT, D])
        xnT = sb("xnT", [P, KD, TG])
        wh = sb("wh", [P, 2, GT, WX])
        ej_diag = sb("ej_diag", [P, GT, N])
        score = sb("score", [P, GT, N])
        leaky = sb("leaky", [P, GT, N])
        mask = sb("mask", [P, GT, N])
        masked = sb("masked", [P, GT, N])
        centred = sb("centred", [P, GT, N])
        row_max = sb("row_max", [P, GT])
        row_sum = sb("row_sum", [P, GT])
        row_inv = sb("row_inv", [P, GT])
        probs = sb("probs", [P, GT, N])
        block_probs = sb("block_probs", [P, GT, P])
        probsT = sb("probsT", [P, GT, P])
        exp_z = sb("exp_z", [P, 2, 2 * D])
        relu_x = sb("relu_x", [P, 2, 2 * D])
        x2 = sb("x2", [P, 2, GT, D])
        xn2 = sb("xn2", [P, 2, GT, D])
        xn2T = sb("xn2T", [P, 2, KD, TG])
        gt = sb("gt", [P, GT, E, E])
        ge = sb("ge", [P, GT, E, E])
        rank = sb("rank", [P, GT, E])
        chosen = sb("chosen", [P, GT * E], BF16)
        stash = sb("stash", [P, ST])
        pos_e = sb("pos_e", [P, GT * E])
        pos_tmp = sb("pos_tmp", [P, 2, GT * E])
        free_row = sb("free_row", [P, E])
        scatter_row = sb("scatter_row", [P, 2, 2 * GT], U32)
        count = sb("count", [P, E])
        count_i = sb("count_i", [P, E], I32)
        tiles_i = sb("tiles_i", [P, E], I32)
        tiles = sb("tiles", [P, E])
        sums = sb("sums", [P, 4, E])
        first_tile = sb("first_tile", [P, E])
        offset = sb("offset", [P, E])
        pad_f = sb("pad_f", [P, E])
        pad_row = sb("pad_row", [P, E], U32)
        big = [sb(f"big{i}", [P, NB * E]) for i in range(3)]
        tab = sb("tab", [P, 4, NB])
        v_top = sb("v_top", [P, NG, 2, GT])
        small = sb("small", [P, 3, NG * GT])

        ps_T = psum("ps_T", [P, KD, TG])
        ps_W = psum("ps_W", [P, 2, 512])
        ps_E = psum("ps_E", [P, 512])
        ps_P = psum("ps_P", [P, GT, P])
        ps_Z = psum("ps_Z", [P, 2, 2 * D])
        E_SC, E_L, E_R, E_TOT = (ps_E[:, s:e] for s, e in ((0, GT * N), (256, 288), (288, 320), (320, 328)))

        names = ("a_const a_const2 a_wload a_wext mv1_ready ln1_ready xn_ready xnT_ready xnT_copied wh_ready "
                 "wh_copied diag_ready score_ready score_read centred_ready exp_ready probs_ready probsT_ready "
                 "probsT_copied z_ready expz_ready relu_ready x2_ready mv2_ready ln2_ready "
                 "xn2_ready xn2T_ready xn2T_copied logits_ready chosen_ready prefix_ready "
                 "rows_ready pad_ready padded gap_ready gapexp_ready "
                 "c_stats1 c_softmax c_probs c_elu c_rank c_pos c_mid c_ln1 c_ln2 c_setup c_psetup dve_held pool_held")
        S = {n: sem(n) for n in names.split()}
        for n in "a_xin a_adjin x2_stored xT_stored scattered".split():
            S[n] = [sem(n + "_even"), sem(n + "_odd")]
        x_g = x.rearrange("(g t p) d -> p g t d", p=P, t=GT)
        adj_g = adj.rearrange("(g t p) j -> p g t j", p=P, t=GT)
        x2_g = x2_dram.rearrange("(g t p) d -> p g t d", p=P, t=GT)

        def one(ap, g):
            return ap[:, g] if isinstance(g, int) else ap[:, bass.ds(g, 1)].rearrange("p o t d -> p (o t) d")

        block = ctx.enter_context(nc.Block())

        def rounds(eng, body):
            for i in range(-1, 3):
                body(i, i % 2)
            with eng.Fori(0, (NG - 4) // 2) as n:
                for u in range(2):
                    i = n * 2 + (3 + u)
                    body(i, (3 + u) % 2)
            for i in range(NG - 1, NG + 1):
                body(i, i % 2)

        @block.sync
        def _(sp):
            sp.dma_start(w_ext[:, :, 0:D], W.rearrange("(k p) f -> p k f", p=P)).then_inc(S["a_wload"], 16)
            sp.dma_start(a_rows[:], a.rearrange("(o s f) u -> o s (f u)", o=1, s=2).to_broadcast([P, 2, D])).then_inc(S["a_wload"], 16)
            sp.dma_start(gw[:], gate_wT).then_inc(S["a_wload"], 16)
            for g in range(2):
                sp.dma_start(x_sb[:, g], one(x_g, g)).then_inc(S["a_xin"][g], 32)
                sp.dma_start(adj_sb[:, g], one(adj_g, g)).then_inc(S["a_adjin"][g], 32)

            def body(i, par):
                if inside(i, NG):
                    if inside(i + 2, NG):
                        sp.wait_ge(S["relu_ready"], i * 2 + 2)
                        sp.dma_start(x_sb[:, par], one(x_g, i + 2)).then_inc(S["a_xin"][par], 32)
                        sp.wait_ge(S["centred_ready"], i + 1)
                        sp.dma_start(adj_sb[:, par], one(adj_g, i + 2)).then_inc(S["a_adjin"][par], 32)
                    sp.wait_ge(S["mv2_ready"], i + 1)
                    sp.dma_start(one(x2_g, i), x2[:, par]).then_inc(S["x2_stored"][par], 32)
                if inside(i - 1, NG):
                    sp.wait_ge(S["xn2T_copied"], i)
                    sp.dma_start(one(xT_dram, i - 1), xn2T[:, 1 - par]).then_inc(S["xT_stored"][1 - par], 32)

            for i in range(-1, 2):
                body(i, i % 2)
            with sp.Fori(0, (NG - 4) // 2) as n:
                for u in range(2):
                    body(n * 2 + (2 + u), (2 + u) % 2)
            for i in range(NG - 2, NG + 1):
                body(i, i % 2)
            for par in range(2):
                sp.wait_ge(S["x2_stored"][par], through(NG - 2 + par, par, 16))
                sp.wait_ge(S["xT_stored"][par], through(NG - 2 + par, par, 16))

        @block.gpsimd
        def _(pool):
            ch = Chain(pool, S["c_psetup"], 0)
            ch.step(pool.memset(ident[:], 0.0))
            ch.step(pool.memset(node_of[:], 0.0))
            ch.step(pool.memset(before_f[:], 1.0))
            ch.step(pool.memset(lower_e[:], 1.0))
            ch.step(pool.memset(half[:], -0.5))
            ch.step(pool.memset(zero_rows[:], 0.0))
            ch.step(pool.memset(block_probs[:], 0.0))
            ch.step(pool.memset(ones_b[:], 1.0))
            ch.step(pool.iota(exp_base_i[:], pattern=[[REG, E]], base=0, channel_multiplier=0))
            ch.step(pool.iota(lane_i[:], pattern=[[1, 1]], base=0, channel_multiplier=1))
            ch.step(pool.iota(jrow_i[:], pattern=[[1, NB]], base=0, channel_multiplier=0))
            ch.wait()
            ch.step(pool.affine_select(out=ident[:], in_=ident[:], compare_op=ALU.not_equal, fill=1.0, base=0,
                                       pattern=[[-1, P]], channel_multiplier=1))
            ch.step(pool.affine_select(out=node_of[:], in_=node_of[:], compare_op=ALU.not_equal, fill=1.0, base=0,
                                       pattern=[[-1, N]], channel_multiplier=1))
            ch.step(pool.affine_select(out=before_f[:], in_=before_f[:], compare_op=ALU.is_gt, fill=0.0, base=0,
                                       pattern=[[1, P]], channel_multiplier=-1))
            ch.step(pool.affine_select(out=lower_e[:], in_=lower_e[:], compare_op=ALU.is_gt, fill=0.0, base=0,
                                       pattern=[[1, E], [-1, E]], channel_multiplier=0))
            ch.wait()
            ch.step(pool.affine_select(out=node_of[:], in_=node_of[:], compare_op=ALU.not_equal, fill=1.0, base=-N,
                                       pattern=[[-1, N]], channel_multiplier=1))
            ch.wait()
            pool.tensor_copy(before[:], before_f[:]).then_inc(S["a_const"], 1)

            def layer_norm(g, par, mv, var_eps, rstd, prod, shift, c, ready, used, mv_ready):
                ch = Chain(pool, S[c], g * 3)
                pool.wait_ge(S[mv_ready], g + 1)
                wait_if(pool, S[used], g - 1)
                hold(pool, S["pool_held"])
                ch.step(pool.tensor_scalar(var_eps[:], mv[:, par, :, 1], EPS, None, ALU.add))
                ch.wait()
                ch.step(pool.tensor_tensor(rstd[:, par], var_eps[:], half[:], ALU.pow))
                ch.wait()
                ch.step(pool.tensor_tensor(prod[:], mv[:, par, :, 0], rstd[:, par], ALU.mult))
                ch.wait()
                hold(pool, S["pool_held"])
                pool.tensor_scalar(shift[:, par], prod[:], -1.0, None, ALU.mult).then_inc(S[ready], 1)

            def body(i, par):
                if inside(i + 1, NG):
                    layer_norm(i + 1, 1 - par, mv1, var_eps1, rstd1, prod1, shift1, "c_ln1", "ln1_ready", "xn_ready", "mv1_ready")
                if inside(i - 1, NG):
                    pool.wait_ge(S["rows_ready"], i)
                    hold(pool, S["pool_held"])
                    for s in range(2):
                        for t in range(GT):
                            c = s * GT + t
                            pool.indirect_dma_start(
                                out=regions, out_offset=bass.IndirectOffsetOnAxis(ap=scatter_row[:, 1 - par, c:c + 1], axis=0),
                                in_=xn2[:, 1 - par, t, :], in_offset=None).then_inc(S["scattered"][1 - par], 32)
                if inside(i, NG):
                    layer_norm(i, par, mv2, var_eps2, rstd2, prod2, shift2, "c_ln2", "ln2_ready", "xn2_ready", "mv2_ready")

            rounds(pool, body)
            pool.wait_ge(S["pad_ready"], 1)
            for e in range(E):
                pool.indirect_dma_start(
                    out=regions, out_offset=bass.IndirectOffsetOnAxis(ap=pad_row[:, e:e + 1], axis=0),
                    in_=zero_rows[:], in_offset=None).then_inc(S["padded"], 16)
            pool.wait_ge(S["padded"], 16 * E)
            for par in range(2):
                pool.wait_ge(S["scattered"][par], through(NG - 2 + par, par, 16 * 2 * GT))

        @block.scalar
        def _(act):
            def normed(g, par, dst, src, rstd, shift, ln_ready, ready):
                act.wait_ge(S[ln_ready], g + 1)
                for t in range(GT):
                    last = act.activation(dst[:, t], src[:, par, t], ACT.Identity,
                                          bias=shift[:, par, t:t + 1], scale=rstd[:, par, t:t + 1])
                last.then_inc(S[ready], 1)

            def body(i, par):
                X, Y, Z = i + 1, i, i - 1
                hasX, hasY, hasZ = inside(X, NG), inside(Y, NG), inside(Z, NG)
                if hasZ:
                    wait_if(act, S["xn2T_ready"], Z - 1)
                    wait_if(act, S["scattered"][1 - par], through(Z - 2, 1 - par, 16 * 2 * GT))
                    normed(Z, 1 - par, xn2[:, 1 - par], x2, rstd2, shift2, "ln2_ready", "xn2_ready")
                if hasX:
                    wait_if(act, S["xnT_ready"], X)
                    normed(X, 1 - par, xn, x_sb, rstd1, shift1, "ln1_ready", "xn_ready")
                if hasY:
                    act.wait_ge(S["centred_ready"], Y + 1)
                    act.activation(probs[:], centred[:], ACT.Exp).then_inc(S["exp_ready"], 1)
                if hasZ:
                    act.wait_ge(S["xn2T_ready"], Z + 1)
                    wait_if(act, S["logits_ready"], Z - 1)
                    wait_if(act, S["xT_stored"][1 - par], through(Z - 2, 1 - par, 16))
                    for k in range(KD):
                        last = act.copy(xn2T[:, 1 - par, k], ps_T[:, k])
                    last.then_inc(S["xn2T_copied"], 1)
                if hasX:
                    act.wait_ge(S["xnT_ready"], X + 1)
                    wait_if(act, S["wh_ready"], X * GT)
                    for k in range(KD):
                        last = act.copy(xnT[:, k], ps_T[:, k])
                    last.then_inc(S["xnT_copied"], 1)
                if hasX:
                    wait_if(act, S["z_ready"], (X - 1) * 2)
                    for t in range(GT):
                        act.wait_ge(S["wh_ready"], X * GT + (t + 1))
                        act.copy(wh[:, 1 - par, t], ps_W[:, t % 2, 0:WX]).then_inc(S["wh_copied"], 1)
                if hasY:
                    act.wait_ge(S["probsT_ready"], Y + 1)
                    wait_if(act, S["z_ready"], Y * 2)
                    act.copy(probsT[:], ps_P[:]).then_inc(S["probsT_copied"], 1)
                if hasY:
                    for h in range(2):
                        act.wait_ge(S["z_ready"], Y * 2 + (h + 1))
                        wait_if(act, S["x2_ready"], (Y - 1) * 2 + (h + 1))
                        act.activation(exp_z[:, h], ps_Z[:, h], ACT.Exp).then_inc(S["expz_ready"], 1)

            rounds(act, body)
            act.wait_ge(S["gap_ready"], 1)
            act.activation(small[:, 1], small[:, 0], ACT.Exp).then_inc(S["gapexp_ready"], 1)

        @block.tensor
        def _(pe):
            pe.wait_ge(S["a_const"], 1)
            pe.wait_ge(S["a_wext"], 1)

            def next_of(g):
                return min(g + 2, NG) if isinstance(g, int) else g + 2

            def body(i, par):
                X, Y, Z = i + 1, i, i - 1
                hasX, hasY, hasZ = inside(X, NG), inside(Y, NG), inside(Z, NG)
                if hasZ:
                    pe.wait_ge(S["xn2_ready"], Z + 1)
                    pe.wait_ge(S["xnT_copied"], next_of(Z))
                    for k in range(KD):
                        for t in range(GT):
                            last = pe.transpose(ps_T[:, k, t * P:(t + 1) * P], xn2[:, 1 - par, t, k * P:(k + 1) * P], ident[:])
                    last.then_inc(S["xn2T_ready"], 1)
                if hasY:
                    pe.wait_ge(S["diag_ready"], Y + 1)
                    pe.matmul(E_SC, same_graph[:], ej_diag[:].rearrange("p t j -> p (t j)"),
                              start=True, stop=True).then_inc(S["score_ready"], 1)
                if hasX:
                    pe.wait_ge(S["xn_ready"], X + 1)
                    wait_if(pe, S["xn2T_copied"], X - 1)
                    for k in range(KD):
                        for t in range(GT):
                            last = pe.transpose(ps_T[:, k, t * P:(t + 1) * P], xn[:, t, k * P:(k + 1) * P], ident[:])
                    last.then_inc(S["xnT_ready"], 1)
                if hasZ:
                    pe.wait_ge(S["xn2T_copied"], Z + 1)
                    pe.wait_ge(S["score_read"], next_of(Z))
                    wait_if(pe, S["chosen_ready"], Z)
                    for t in range(GT):
                        for k in range(KD):
                            last = pe.matmul(E_L[:, t * E:(t + 1) * E], xn2T[:, 1 - par, k, t * P:(t + 1) * P], gw[:, k],
                                             start=(k == 0), stop=(k == KD - 1))
                    last.then_inc(S["logits_ready"], 1)
                if hasX:
                    pe.wait_ge(S["xnT_copied"], X + 1)
                    for t in range(GT):
                        if t >= 2:
                            pe.wait_ge(S["wh_copied"], X * GT + (t - 1))
                        else:
                            wait_if(pe, S["wh_copied"], X * GT + (t - 1))
                        for k in range(KD):
                            last = pe.matmul(ps_W[:, t % 2, 0:WX], xnT[:, k, t * P:(t + 1) * P], w_ext[:, k],
                                             start=(k == 0), stop=(k == KD - 1))
                        last.then_inc(S["wh_ready"], 1)
                if hasY:
                    pe.wait_ge(S["probs_ready"], Y + 1)
                    wait_if(pe, S["probsT_copied"], Y)
                    for t in range(GT):
                        last = pe.transpose(ps_P[:, t], block_probs[:, t], ident[:])
                    last.then_inc(S["probsT_ready"], 1)
                if hasZ:
                    pe.wait_ge(S["chosen_ready"], Z + 1)
                    pe.matmul(E_R, before[:], chosen[:], start=True, stop=False)
                    for t in range(1, GT):
                        pe.matmul(E_R[:, t * E:], ones_b[:], chosen[:, 0:(GT - t) * E], start=False, stop=(t == GT - 1))
                    for t in range(GT):
                        last = pe.matmul(E_TOT, ones_b[:], chosen[:, t * E:(t + 1) * E], start=(t == 0), stop=(t == GT - 1))
                    last.then_inc(S["prefix_ready"], 1)
                if hasY:
                    pe.wait_ge(S["probsT_copied"], Y + 1)
                    for t in range(GT):
                        if t % 2 == 0:
                            wait_if(pe, S["expz_ready"], (Y - 1) * 2 + (t // 2 + 1))
                            wait_if(pe, S["relu_ready"], (Y - 1) * 2 + (t // 2 + 1))
                        last = pe.matmul(ps_Z[:, t // 2, (t % 2) * D:(t % 2 + 1) * D], probsT[:, t], wh[:, par, t, 0:D],
                                         start=True, stop=True)
                        if t % 2 == 1:
                            last.then_inc(S["z_ready"], 1)

            rounds(pe, body)

        @block.vector
        def _(dve):
            ch = Chain(dve, S["c_setup"], 0)
            ch.step(dve.memset(same_graph[:], 0.0))
            ch.wait()
            ch.step(dve.memset(same_graph[0:N, 0:N], 1.0))
            ch.step(dve.memset(same_graph[N:P, N:P], 1.0))
            dve.wait_ge(S["a_wload"], 48)
            for k in range(KD):
                for s in range(2):
                    ch.step(dve.tensor_tensor_reduce(wa_tmp[:], w_ext[:, k, 0:D], a_rows[:, s], 1.0, 0.0, ALU.mult, ALU.add,
                                                     w_ext[:, k, D + s:D + s + 1]))
                    ch.wait()
            dve.wait_ge(S["a_const"], 1)
            ch.step(dve.tensor_copy(exp_base[:], exp_base_i[:]))
            ch.step(dve.tensor_copy(free_row[:], exp_base_i[:]))
            ch.step(dve.tensor_copy(lane[:], lane_i[:]))
            ch.step(dve.tensor_copy(jrow[:], jrow_i[:]))
            ch.wait()
            ch.step(dve.tensor_scalar(jrow128[:], jrow[:], float(P), None, ALU.mult))
            ch.wait()
            dve.memset(wa_tmp[:, 0:1], 0.0).then_inc(S["a_wext"], 1)

            def spread(ap, n):
                return ap.unsqueeze(2).to_broadcast([P, GT, n])

            def stats(g, par):
                ch = Chain(dve, S["c_stats1"], g * GT)
                dve.wait_ge(S["a_xin"][par], through(g, par, 16))
                for t in range(GT):
                    ch.step(dve.bn_stats(stats1[:, t], x_sb[:, par, t]))
                ch.wait()
                wait_if(dve, S["ln1_ready"], g - 1)
                hold(dve, S["dve_held"])
                for t in range(GT):
                    last = dve.bn_aggr(mv1[:, par, t], stats1[:, t])
                last.then_inc(S["mv1_ready"], 1)

            def diag(g, par):
                dve.wait_ge(S["wh_copied"], (g + 1) * GT)
                dve.tensor_tensor(ej_diag[:], node_of[:].unsqueeze(1).to_broadcast([P, GT, N]),
                                  wh[:, par, :, D + 1:D + 2].to_broadcast([P, GT, N]), ALU.mult).then_inc(S["diag_ready"], 1)

            def softmax_in(g, par):
                ch = Chain(dve, S["c_softmax"], g * 4)
                dve.wait_ge(S["a_adjin"][par], through(g, par, 16))
                ch.step(dve.tensor_scalar(mask[:], adj_sb[:, par], 0.0, MASK, ALU.is_equal, ALU.mult))
                dve.wait_ge(S["score_ready"], g + 1)
                dve.tensor_tensor(score[:], E_SC.rearrange("p (t j) -> p t j", t=GT),
                                  wh[:, par, :, D:D + 1].to_broadcast([P, GT, N]), ALU.add).then_inc(S["score_read"], 1)
                dve.wait_ge(S["score_read"], g + 1)
                ch.step(dve.scalar_tensor_tensor(out=leaky[:], in0=score[:], scalar=SLOPE, in1=score[:], op0=ALU.mult, op1=ALU.max))
                ch.wait()
                ch.step(dve.tensor_tensor(masked[:], leaky[:], mask[:], ALU.add))
                ch.wait()
                ch.step(dve.tensor_reduce(row_max[:], masked[:], AX.X, ALU.max))
                ch.wait()
                dve.tensor_tensor(centred[:], masked[:], spread(row_max[:], N), ALU.subtract).then_inc(S["centred_ready"], 1)

            def softmax_out(g):
                ch = Chain(dve, S["c_probs"], g * 2)
                dve.wait_ge(S["exp_ready"], g + 1)
                ch.step(dve.tensor_reduce(row_sum[:], probs[:], AX.X, ALU.add))
                ch.wait()
                ch.step(dve.reciprocal(row_inv[:], row_sum[:]))
                ch.wait()
                wait_if(dve, S["probsT_ready"], g)
                for h in range(2):
                    r = slice(h * N, (h + 1) * N)
                    last = dve.tensor_tensor(block_probs[r, :, h * N:(h + 1) * N], probs[r],
                                             row_inv[r].unsqueeze(2).to_broadcast([N, GT, N]), ALU.mult)
                last.then_inc(S["probs_ready"], 1)

            def elu_add(g, par):
                ch = Chain(dve, S["c_elu"], g * GT)
                wait_if(dve, S["xn2_ready"], g - 1)
                wait_if(dve, S["x2_stored"][par], through(g - 2, par, 16))
                for h in range(2):
                    ts = slice(2 * h, 2 * h + 2)
                    dve.wait_ge(S["expz_ready"], g * 2 + (h + 1))
                    dve.scalar_tensor_tensor(out=relu_x[:, h], in0=ps_Z[:, h], scalar=0.0,
                                             in1=x_sb[:, par, ts].rearrange("p t d -> p (t d)"),
                                             op0=ALU.max, op1=ALU.add).then_inc(S["relu_ready"], 1)
                    dve.wait_ge(S["relu_ready"], g * 2 + (h + 1))
                    dve.scalar_tensor_tensor(out=x2[:, par, ts].rearrange("p t d -> p (t d)"), in0=exp_z[:, h], scalar=1.0,
                                             in1=relu_x[:, h], op0=ALU.min, op1=ALU.add).then_inc(S["x2_ready"], 1)
                    dve.wait_ge(S["x2_ready"], g * 2 + (h + 1))
                    for t in range(2 * h, 2 * h + 2):
                        ch.step(dve.bn_stats(stats2[:, t], x2[:, par, t]))
                ch.wait()
                wait_if(dve, S["ln2_ready"], g - 1)
                hold(dve, S["dve_held"])
                for t in range(GT):
                    last = dve.bn_aggr(mv2[:, par, t], stats2[:, t])
                last.then_inc(S["mv2_ready"], 1)

            def choose(g):
                ch = Chain(dve, S["c_rank"], g * 8)
                dve.wait_ge(S["logits_ready"], g + 1)
                L = stash[:, ST_L:ST_L + GT * E].rearrange("p (t e) -> p t e", t=GT)
                ch.step(dve.tensor_copy(stash[:, ST_L:ST_L + GT * E], E_L))
                ch.wait()
                other = L.unsqueeze(2).to_broadcast([P, GT, E, E])
                own = L.unsqueeze(3).to_broadcast([P, GT, E, E])
                ch.step(dve.tensor_tensor(gt[:], other, own, ALU.is_gt))
                ch.step(dve.tensor_tensor(ge[:], other, own, ALU.is_ge))
                ch.wait()
                ch.step(dve.tensor_tensor(ge[:], ge[:], lower_e[:].unsqueeze(1).to_broadcast([P, GT, E, E]), ALU.mult))
                ch.wait()
                ch.step(dve.tensor_tensor(gt[:], gt[:], ge[:], ALU.max))
                ch.wait()
                ch.step(dve.tensor_reduce(rank[:], gt[:], AX.X, ALU.add))
                ch.wait()
                R = rank[:].rearrange("p t e -> p (t e)")
                dve.tensor_scalar(chosen[:], R, 2.0, None, ALU.is_lt).then_inc(S["chosen_ready"], 1)
                for s in range(2):
                    ch.step(dve.tensor_scalar(stash[:, ST_OH + s * GT * E:ST_OH + (s + 1) * GT * E], R, float(s), None, ALU.is_equal))

            def place(g, par):
                ch = Chain(dve, S["c_pos"], g * 5)
                dve.wait_ge(S["c_rank"], (g + 1) * 8)
                dve.wait_ge(S["prefix_ready"], g + 1)
                ch.step(dve.tensor_tensor(pos_e[:].rearrange("p (t e) -> p t e", t=GT), E_R.rearrange("p (t e) -> p t e", t=GT),
                                          free_row[:].unsqueeze(1).to_broadcast([P, GT, E]), ALU.add))
                ch.wait()
                ch.step(dve.tensor_tensor(free_row[:], free_row[:], E_TOT, ALU.add))
                ch.step(dve.tensor_tensor(pos_tmp[:], stash[:, ST_OH:ST_POS].rearrange("p (s c) -> p s c", s=2),
                                          pos_e[:].unsqueeze(1).to_broadcast([P, 2, GT * E]), ALU.mult))
                ch.wait()
                ch.step(dve.tensor_reduce(stash[:, ST_POS:ST], pos_tmp[:].rearrange("p s (t e) -> p (s t) e", e=E), AX.X, ALU.add))
                ch.wait()
                wait_if(dve, S["scattered"][par], through(g - 2, par, 16 * 2 * GT))
                dve.tensor_copy(scatter_row[:, par], stash[:, ST_POS:ST]).then_inc(S["rows_ready"], 1)
                if isinstance(g, int):
                    dst = stash_all[:, g]
                else:
                    dst = stash_all[:, bass.ds(g, 1)].rearrange("p o c -> p (o c)")
                ch.step(dve.tensor_copy(dst, stash[:]))
                ch.wait()

            def body(i, par):
                X, Y, Z = i + 1, i, i - 1
                hasX, hasY, hasZ = inside(X, NG), inside(Y, NG), inside(Z, NG)
                if hasY:
                    diag(Y, par)
                if hasX:
                    stats(X, 1 - par)
                if hasY:
                    softmax_in(Y, par)
                if hasZ:
                    choose(Z)
                if hasY:
                    softmax_out(Y)
                if hasZ:
                    place(Z, 1 - par)
                if hasY:
                    elu_add(Y, par)

            rounds(dve, body)

            ch = Chain(dve, S["c_mid"], 0)

            def do(ins):
                ch.step(ins)
                ch.wait()

            do(dve.tensor_tensor(count[:], free_row[:], exp_base[:], ALU.subtract))
            do(dve.tensor_scalar(pad_f[:], free_row[:], lane[:, 0:1], None, ALU.add))
            dve.tensor_copy(pad_row[:], pad_f[:]).then_inc(S["pad_ready"], 1)
            do(dve.tensor_scalar(count_i[:], count[:], float(P - 1), None, ALU.add))
            do(dve.tensor_scalar(tiles_i[:], count_i[:], 7, None, ALU.logical_shift_right))
            do(dve.tensor_copy(tiles[:], tiles_i[:]))
            do(dve.tensor_copy(sums[:, 0], tiles_i[:]))
            for n, d in enumerate((1, 2, 4)):
                do(dve.tensor_copy(sums[:, n + 1, 0:d], sums[:, n, 0:d]))
                do(dve.tensor_tensor(sums[:, n + 1, d:E], sums[:, n, d:E], sums[:, n, 0:E - d], ALU.add))
            end_tile = sums[:, 3]
            do(dve.tensor_tensor(first_tile[:], end_tile, tiles[:], ALU.subtract))
            do(dve.scalar_tensor_tensor(out=offset[:], in0=first_tile[:], scalar=-float(P), in1=exp_base[:], op0=ALU.mult, op1=ALU.add))
            b = [t[:].rearrange("p (j e) -> p j e", e=E) for t in big]

            def by_e(ap):
                return ap.unsqueeze(1).to_broadcast([P, NB, E])

            def by_j(ap):
                return ap.unsqueeze(2).to_broadcast([P, NB, E])

            do(dve.tensor_tensor(b[0], by_j(jrow[:]), by_e(first_tile[:]), ALU.is_ge))
            do(dve.tensor_tensor(b[1], by_j(jrow[:]), by_e(end_tile), ALU.is_ge))
            do(dve.tensor_tensor(b[0], b[0], b[1], ALU.subtract))
            do(dve.tensor_tensor(b[2], by_j(jrow128[:]), by_e(offset[:]), ALU.add))
            do(dve.tensor_tensor(b[2], b[2], b[0], ALU.mult))
            do(dve.tensor_reduce(tab[:, 0], b[2], AX.X, ALU.add))
            do(dve.tensor_reduce(tab[:, 1], b[1], AX.X, ALU.add))
            do(dve.tensor_scalar(tab[:, 2], b[1][:, :, E - 1], float((E - 1) * REG), None, ALU.mult))
            do(dve.tensor_tensor(tile_row[:], tab[:, 0], tab[:, 2], ALU.add))
            do(dve.tensor_scalar(tile_exp[:], tab[:, 1], float(E - 1), None, ALU.min))
            oh = stash_all[:, :, ST_OH:ST_POS].rearrange("p g (c e) -> p g c e", e=E)
            flat = big[0][:, 0:NG * 2 * GT * E]
            do(dve.tensor_tensor(flat.rearrange("p (g c e) -> p g c e", e=E, g=NG), oh,
                                 offset[:].unsqueeze(1).unsqueeze(1).to_broadcast([P, NG, 2 * GT, E]), ALU.mult))
            do(dve.tensor_reduce(big[1][:, 0:NG * 2 * GT], flat.rearrange("p (q e) -> p q e", e=E), AX.X, ALU.add))
            do(dve.tensor_tensor(row_of[:], stash_all[:, :, ST_POS:ST],
                                 big[1][:, 0:NG * 2 * GT].rearrange("p (g c) -> p g c", g=NG), ALU.subtract))
            for s in range(2):
                do(dve.tensor_tensor(flat[:, 0:NG * GT * E].rearrange("p (g c) -> p g c", g=NG),
                                     stash_all[:, :, ST_OH + s * GT * E:ST_OH + (s + 1) * GT * E],
                                     stash_all[:, :, ST_L:ST_L + GT * E], ALU.mult))
                do(dve.tensor_reduce(v_top[:, :, s], flat[:, 0:NG * GT * E].rearrange("p (g t e) -> p g t e", g=NG, e=E), AX.X, ALU.add))
            sm = small[:].rearrange("p s (g t) -> p s g t", g=NG)
            dve.tensor_tensor(sm[:, 0], v_top[:, :, 1], v_top[:, :, 0], ALU.subtract).then_inc(S["gap_ready"], 1)
            dve.wait_ge(S["gapexp_ready"], 1)
            do(dve.tensor_scalar(small[:, 2], small[:, 1], 1.0, None, ALU.add))
            do(dve.reciprocal(small[:, 0], small[:, 2]))
            do(dve.tensor_copy(weight_of[:, :, 0:GT], sm[:, 0]))
            do(dve.tensor_tensor(weight_of[:, :, GT:2 * GT], sm[:, 1], sm[:, 0], ALU.mult))


def part_b(nc, top, sem, v):
    experts, E, D, KD, H, KH, WC, NB = (v[k] for k in ("experts", "E", "D", "KD", "H", "KH", "WC", "NB"))
    ident, tile_row, tile_exp, regions, y_dram = (v[k] for k in ("ident", "tile_row", "tile_exp", "regions", "y_dram"))
    REG = v["REG"]
    with ExitStack() as ctx:
        def sb(name, shape, dt=F32):
            return ctx.enter_context(nc.sbuf_tensor(name, shape, dt))

        def psum(name, shape):
            return ctx.enter_context(nc.psum_tensor(name, shape, F32))

        w_raw = sb("w_raw", [P, 2, 2 * WC])
        w_hi = sb("w_hi", [P, E * 2 * WC], F32R)
        w_lo = sb("w_lo", [P, E * 2 * WC], F32R)
        rows = sb("rows", [P, 2, D])
        xT_hi = sb("xT_hi", [P, 2, KD, P], F32R)
        xT_lo = sb("xT_lo", [P, 2, KD, P], F32R)
        hid = sb("hid", [P, 2, H])
        hT_hi = sb("hT_hi", [P, 2, KH, P], F32R)
        hT_lo = sb("hT_lo", [P, 2, KH, P], F32R)
        y_sb = sb("y_sb", [P, 2, D])
        ps_X = psum("ps_X", [P, 512])
        ps_H = psum("ps_H", [P, 2, H])
        ps_HT = psum("ps_HT", [P, 2, KH, P])
        ps_Y = psum("ps_Y", [P, 2, 512])

        names = ("w_split_hi w_split xT_ready xhi_ready xlo_ready h_ready silu_ready hT_ready "
                 "hhi_ready hlo_ready y_ready y_copied")
        S = {n: sem("b_" + n) for n in names.split()}
        for n in "w_loaded rows_loaded y_stored".split():
            S[n] = [sem(f"b_{n}_even"), sem(f"b_{n}_odd")]
        block = ctx.enter_context(nc.Block())

        def steps(eng, body):
            for j in range(-1, 4):
                body(j, j % 2)
            with eng.Fori(0, (NB - 6) // 2) as n:
                for u in range(2):
                    body(n * 2 + (4 + u), u)
            for j in range(NB - 2, NB + 2):
                body(j, j % 2)

        @block.sync
        def _(sp):
            def load(j, par):
                r = sp.value_load(tile_row[0:1, bass.ds(j, 1)], min_val=0, max_val=E * REG - P)
                sp.dma_start(rows[:, par], regions[bass.ds(r, P), :]).then_inc(S["rows_loaded"][par], 32)

            def body(j, par):
                if inside(j + 2, NB) and (not isinstance(j, int) or j >= 0):
                    sp.wait_ge(S["xT_ready"], j + 1)
                    load(j + 2, par)
                if inside(j - 2, NB):
                    sp.wait_ge(S["y_copied"], j - 1)
                    row = (j - 2) * P
                    dst = y_dram[row:row + P] if isinstance(j, int) else y_dram[bass.ds(row, P)]
                    sp.dma_start(dst, y_sb[:, par]).then_inc(S["y_stored"][par], 32)

            load(0, 0)
            load(1, 1)
            steps(sp, body)
            for par in range(2):
                sp.wait_ge(S["y_stored"][par], through(NB - 2 + par, par, 16))

        @block.gpsimd
        def _(pool):
            for e in range(2):
                pool.dma_start(w_raw[:, e], experts[:, e]).then_inc(S["w_loaded"][e], 16)
            for e in range(E):
                c = slice(e * 2 * WC, (e + 1) * 2 * WC)
                pool.wait_ge(S["w_loaded"][e % 2], 16 * (e // 2 + 1))
                pool.tensor_copy(w_hi[:, c], w_raw[:, e % 2]).then_inc(S["w_split_hi"], 1)
                pool.wait_ge(S["w_split_hi"], e + 1)
                pool.tensor_tensor(w_lo[:, c], w_raw[:, e % 2], w_hi[:, c].bitcast(F32), ALU.subtract).then_inc(S["w_split"], 1)
                if e + 2 < E:
                    pool.wait_ge(S["w_split"], e + 1)
                    pool.dma_start(w_raw[:, e % 2], experts[:, e + 2]).then_inc(S["w_loaded"][e % 2], 16)

        @block.scalar
        def _(act):
            def body(j, par):
                if inside(j, NB):
                    act.wait_ge(S["h_ready"], j + 1)
                    wait_if(act, S["hT_ready"], j - 1)
                    act.activation(hid[:, par], ps_H[:, par], ACT.Silu).then_inc(S["silu_ready"], 1)
                if inside(j + 1, NB):
                    act.wait_ge(S["xT_ready"], j + 2)
                    wait_if(act, S["h_ready"], j)
                    act.copy(xT_hi[:, 1 - par].rearrange("p k t -> p (k t)"), ps_X[:, 0:D]).then_inc(S["xhi_ready"], 1)
                if inside(j - 1, NB):
                    act.wait_ge(S["hT_ready"], j)
                    wait_if(act, S["y_ready"], j - 2)
                    act.copy(hT_hi[:, 1 - par], ps_HT[:, 1 - par]).then_inc(S["hhi_ready"], 1)

            steps(act, body)

        @block.vector
        def _(dve):
            def body(j, par):
                if inside(j + 1, NB):
                    dve.wait_ge(S["xhi_ready"], j + 2)
                    wait_if(dve, S["h_ready"], j)
                    q = xT_hi[:, 1 - par].rearrange("p k t -> p (k t)")
                    dve.tensor_tensor(xT_lo[:, 1 - par].rearrange("p k t -> p (k t)"), ps_X[:, 0:D], q.bitcast(F32),
                                      ALU.subtract).then_inc(S["xlo_ready"], 1)
                if inside(j - 1, NB):
                    dve.wait_ge(S["hhi_ready"], j)
                    wait_if(dve, S["y_ready"], j - 2)
                    dve.tensor_tensor(hT_lo[:, 1 - par], ps_HT[:, 1 - par], hT_hi[:, 1 - par].bitcast(F32),
                                      ALU.subtract).then_inc(S["hlo_ready"], 1)
                if inside(j - 2, NB):
                    dve.wait_ge(S["y_ready"], j - 1)
                    wait_if(dve, S["y_stored"][par], through(j - 4, par, 16))
                    dve.tensor_copy(y_sb[:, par], ps_Y[:, par, 0:D]).then_inc(S["y_copied"], 1)

            steps(dve, body)

        @block.tensor
        def _(pe):
            def expert_of(j):
                return pe.value_load(tile_exp[0:1, bass.ds(j, 1)], min_val=0, max_val=E - 1)

            def body(j, par):
                if inside(j, NB):
                    e = expert_of(j)
                    pe.wait_ge(S["w_split"], e + 1)
                    pe.wait_ge(S["xhi_ready"], j + 1)
                    pe.wait_ge(S["xlo_ready"], j + 1)
                    wait_if(pe, S["silu_ready"], j - 1)
                    base = pe.snap(e * (2 * WC))
                    n = 0
                    for k in range(KD):
                        for lhs, rhs in ((xT_hi, w_hi), (xT_lo, w_hi), (xT_hi, w_lo)):
                            last = pe.matmul(ps_H[:, par], lhs[:, par, k], rhs[:, bass.ds(base + k * H, H)],
                                             start=(n == 0), stop=(n == 3 * KD - 1))
                            n += 1
                    last.then_inc(S["h_ready"], 1)
                if inside(j - 1, NB):
                    pe.wait_ge(S["silu_ready"], j)
                    wait_if(pe, S["hlo_ready"], j - 2)
                    for k in range(KH):
                        last = pe.transpose(ps_HT[:, 1 - par, k], hid[:, 1 - par, k * P:(k + 1) * P], ident[:])
                    last.then_inc(S["hT_ready"], 1)
                if inside(j + 1, NB):
                    pe.wait_ge(S["rows_loaded"][1 - par], through(j + 1, 1 - par, 16))
                    wait_if(pe, S["xlo_ready"], j + 1)
                    for k in range(KD):
                        last = pe.transpose(ps_X[:, k * P:(k + 1) * P], rows[:, 1 - par, k * P:(k + 1) * P], ident[:])
                    last.then_inc(S["xT_ready"], 1)
                if inside(j - 2, NB):
                    pe.wait_ge(S["hlo_ready"], j - 1)
                    wait_if(pe, S["y_copied"], j - 3)
                    e = expert_of(j - 2)
                    base = pe.snap(e * (2 * WC) + WC)
                    n = 0
                    for k in range(KH):
                        for lhs, rhs in ((hT_hi, w_hi), (hT_lo, w_hi), (hT_hi, w_lo)):
                            last = pe.matmul(ps_Y[:, par, 0:D], lhs[:, par, k], rhs[:, bass.ds(base + k * D, D)],
                                             start=(n == 0), stop=(n == 3 * KH - 1))
                            n += 1
                    last.then_inc(S["y_ready"], 1)

            steps(pe, body)


def part_c(nc, top, sem, v):
    shared, D, KD, H, KH, WC, NG, GT, TG = (v[k] for k in ("shared", "D", "KD", "H", "KH", "WC", "NG", "GT", "TG"))
    row_of, weight_of, y_dram, x2_dram, xT_dram, out = (v[k] for k in ("row_of", "weight_of", "y_dram", "x2_dram", "xT_dram", "out"))
    with ExitStack() as ctx:
        def sb(name, shape, dt=F32):
            return ctx.enter_context(nc.sbuf_tensor(name, shape, dt))

        def psum(name, shape):
            return ctx.enter_context(nc.psum_tensor(name, shape, F32))

        s_raw = sb("s_raw", [P, 3 * WC])
        s_hi = sb("s_hi", [P, 3, WC], F32R)
        s_lo = sb("s_lo", [P, 3, WC], F32R)
        xT = sb("xT", [P, 2, KD, TG])
        xT_h = sb("xT_h", [P, 2, KD, TG], F32R)
        xT_l = sb("xT_l", [P, 2, KD, TG], F32R)
        x2_in = sb("x2_in", [P, 2, GT, D])
        gate = sb("gate", [P, 2, TG])
        hidT = sb("hidT", [P, 2, TG])
        hidT_h = sb("hidT_h", [P, 2, KH, TG], F32R)
        hidT_l = sb("hidT_l", [P, 2, KH, TG], F32R)
        rows_l = sb("rows_l", [P, 2, 2 * GT], U32)
        weights_l = sb("weights_l", [P, 2, 2 * GT])
        y_in = sb("y_in", [P, 2, 2, GT, D])
        out_sb = sb("out_sb", [P, 2, GT, D])
        ps_G = psum("ps_G", [P, 2, TG])
        ps_U = psum("ps_U", [P, 2, TG])
        ps_D = psum("ps_D", [P, 2, 2, D])

        names = ("s_loaded s_hi_ready s_split xhi_ready xlo_ready gate_ready up_ready silu_ready "
                 "hid_ready hhi_ready hlo_ready down_ready idx_ready first_ready out_ready c_comb held")
        S = {n: sem("c_" + n) for n in names.split()}
        for n in "xT_loaded x2_loaded gathered stored".split():
            S[n] = [sem(f"c_{n}_even"), sem(f"c_{n}_odd")]
        x2_g = x2_dram.rearrange("(g t p) d -> p g t d", p=P, t=GT)
        out_g = out.rearrange("(g t p) d -> p g t d", p=P, t=GT)

        def one(ap, g):
            return ap[:, g] if isinstance(g, int) else ap[:, bass.ds(g, 1)].rearrange("p o t d -> p (o t) d")

        block = ctx.enter_context(nc.Block())

        def rounds(eng, body):
            for g in range(4):
                body(g, g % 2)
            with eng.Fori(0, (NG - 6) // 2) as n:
                for u in range(2):
                    body(n * 2 + (4 + u), u)
            for g in range(NG - 2, NG + 1):
                body(g, g % 2)

        @block.sync
        def _(sp):
            sp.dma_start(s_raw[:], shared).then_inc(S["s_loaded"], 16)

            def body(g, par):
                if inside(g, NG):
                    wait_if(sp, S["xlo_ready"], g - 1)
                    sp.dma_start(xT[:, par], one(xT_dram, g)).then_inc(S["xT_loaded"][par], 32)
                    wait_if(sp, S["out_ready"], (g - 1) * GT)
                    sp.dma_start(x2_in[:, par], one(x2_g, g)).then_inc(S["x2_loaded"][par], 32)
                if inside(g - 2, NG):
                    sp.wait_ge(S["out_ready"], (g - 1) * GT)
                    sp.dma_start(one(out_g, g - 2), out_sb[:, par]).then_inc(S["stored"][par], 32)

            for g in range(4):
                body(g, g % 2)
            with sp.Fori(0, (NG - 6) // 2) as n:
                for u in range(2):
                    body(n * 2 + (4 + u), u)
            for g in range(NG - 2, NG + 2):
                body(g, g % 2)
            for par in range(2):
                sp.wait_ge(S["stored"][par], through(NG - 2 + par, par, 16))

        @block.gpsimd
        def _(pool):
            def body(g, par):
                if inside(g, NG):
                    pool.wait_ge(S["idx_ready"], g + 1)
                    wait_if(pool, S["out_ready"], (g - 1) * GT)
                    hold(pool, S["held"])
                    for s in range(2):
                        for t in range(GT):
                            c = s * GT + t
                            pool.indirect_dma_start(
                                out=y_in[:, par, s, t], out_offset=None, in_=y_dram,
                                in_offset=bass.IndirectOffsetOnAxis(ap=rows_l[:, par, c:c + 1], axis=0)).then_inc(S["gathered"][par], 32)

            rounds(pool, body)

        @block.scalar
        def _(act):
            act.wait_ge(S["s_loaded"], 16)
            act.copy(s_hi[:].rearrange("p m c -> p (m c)"), s_raw[:]).then_inc(S["s_hi_ready"], 1)

            def split(g, par):
                act.wait_ge(S["xT_loaded"][par], through(g, par, 16))
                wait_if(act, S["up_ready"], (g - 1) * KH)
                act.copy(xT_h[:, par], xT[:, par]).then_inc(S["xhi_ready"], 1)

            split(0, 0)

            def body(g, par):
                if not inside(g, NG):
                    return
                for b in range(KH):
                    act.wait_ge(S["gate_ready"], g * KH + (b + 1))
                    wait_if(act, S["hid_ready"], g * KH + (b - 1))
                    act.activation(gate[:, b % 2], ps_G[:, b % 2], ACT.Silu).then_inc(S["silu_ready"], 1)
                    act.wait_ge(S["hid_ready"], g * KH + (b + 1))
                    if b == 0:
                        wait_if(act, S["down_ready"], (g - 1) * 2)
                    act.copy(hidT_h[:, par, b], hidT[:, b % 2]).then_inc(S["hhi_ready"], 1)
                    if b == 1 and inside(g + 1, NG):
                        split(g + 1, 1 - par)

            rounds(act, body)

        @block.vector
        def _(dve):
            dve.wait_ge(S["s_hi_ready"], 1)
            dve.tensor_tensor(s_lo[:].rearrange("p m c -> p (m c)"), s_raw[:], s_hi[:].rearrange("p m c -> p (m c)").bitcast(F32),
                              ALU.subtract).then_inc(S["s_split"], 1)

            def split(g, par):
                dve.wait_ge(S["xhi_ready"], g + 1)
                wait_if(dve, S["up_ready"], (g - 1) * KH)
                dve.tensor_tensor(xT_l[:, par], xT[:, par], xT_h[:, par].bitcast(F32), ALU.subtract).then_inc(S["xlo_ready"], 1)

            split(0, 0)

            def tables(g, par):
                wait_if(dve, S["gathered"][par], through(g - 2, par, 16 * 2 * GT))
                wait_if(dve, S["out_ready"], (g - 1) * GT)
                r, w = (t[:, g] if isinstance(g, int) else t[:, bass.ds(g, 1)].rearrange("p o c -> p (o c)") for t in (row_of, weight_of))
                dve.tensor_copy(rows_l[:, par], r)
                dve.tensor_copy(weights_l[:, par], w).then_inc(S["idx_ready"], 1)

            def combine(g, par):
                ch = Chain(dve, S["c_comb"], g * GT)
                dve.wait_ge(S["x2_loaded"][par], through(g, par, 16))
                wait_if(dve, S["stored"][par], through(g - 2, par, 16))
                dve.wait_ge(S["gathered"][par], through(g, par, 16 * 2 * GT))
                dve.wait_ge(S["idx_ready"], g + 1)
                for h in range(2):
                    ts = slice(2 * h, 2 * h + 2)
                    dve.wait_ge(S["down_ready"], g * 2 + (h + 1))
                    dve.scalar_tensor_tensor(out=out_sb[:, par, ts], in0=ps_D[:, h], scalar=-1.0, in1=x2_in[:, par, ts],
                                             op0=ALU.add, op1=ALU.add).then_inc(S["first_ready"], 1)
                dve.wait_ge(S["first_ready"], g * 2 + 2)
                for t in range(GT):
                    ch.step(dve.scalar_tensor_tensor(out=out_sb[:, par, t], in0=y_in[:, par, 0, t], scalar=weights_l[:, par, t:t + 1],
                                                     in1=out_sb[:, par, t], op0=ALU.mult, op1=ALU.add))
                ch.wait()
                for t in range(GT):
                    dve.scalar_tensor_tensor(out=out_sb[:, par, t], in0=y_in[:, par, 1, t], scalar=weights_l[:, par, GT + t:GT + t + 1],
                                             in1=out_sb[:, par, t], op0=ALU.mult, op1=ALU.add).then_inc(S["out_ready"], 1)

            def body(g, par):
                if inside(g, NG):
                    tables(g, par)
                    for b in range(KH):
                        dve.wait_ge(S["silu_ready"], g * KH + (b + 1))
                        dve.wait_ge(S["up_ready"], g * KH + (b + 1))
                        dve.tensor_tensor(hidT[:, b % 2], ps_U[:, b % 2], gate[:, b % 2], ALU.mult).then_inc(S["hid_ready"], 1)
                        dve.wait_ge(S["hhi_ready"], g * KH + (b + 1))
                        dve.tensor_tensor(hidT_l[:, par, b], hidT[:, b % 2], hidT_h[:, par, b].bitcast(F32),
                                          ALU.subtract).then_inc(S["hlo_ready"], 1)
                        if b == 1 and inside(g + 1, NG):
                            split(g + 1, 1 - par)
                if inside(g - 1, NG):
                    combine(g - 1, 1 - par)

            rounds(dve, body)

        @block.tensor
        def _(pe):
            pe.wait_ge(S["s_split"], 1)

            def up_product(dst, m, par, b):
                n = 0
                for k in range(KD):
                    col = slice(k * H + b * P, k * H + (b + 1) * P)
                    for lhs, rhs in ((s_hi, xT_h), (s_lo, xT_h), (s_hi, xT_l)):
                        last = nc.tensor.matmul(dst, lhs[:, m, col], rhs[:, par, k], start=(n == 0), stop=(n == 3 * KD - 1))
                        n += 1
                return last

            def body(g, par):
                if inside(g, NG):
                    pe.wait_ge(S["xlo_ready"], g + 1)
                    for b in range(KH):
                        wait_if(pe, S["silu_ready"], g * KH + (b - 1))
                        up_product(ps_G[:, b % 2], 0, par, b).then_inc(S["gate_ready"], 1)
                        wait_if(pe, S["hid_ready"], g * KH + (b - 1))
                        up_product(ps_U[:, b % 2], 1, par, b).then_inc(S["up_ready"], 1)
                if inside(g - 1, NG):
                    G = g - 1
                    pe.wait_ge(S["hlo_ready"], g * KH)
                    for t in range(GT):
                        if t % 2 == 0:
                            wait_if(pe, S["first_ready"], (G - 1) * 2 + (t // 2 + 1))
                        n = 0
                        for k in range(KH):
                            col = slice(t * P, (t + 1) * P)
                            for lhs, rhs in ((hidT_h, s_hi), (hidT_l, s_hi), (hidT_h, s_lo)):
                                last = pe.matmul(ps_D[:, t // 2, t % 2], lhs[:, 1 - par, k, col], rhs[:, 2, k * D:(k + 1) * D],
                                                 start=(n == 0), stop=(n == 3 * KH - 1))
                                n += 1
                        if t % 2 == 1:
                            last.then_inc(S["down_ready"], 1)

            rounds(pe, body)


def kernel(**inputs):
    import numpy as np
    import concourse.bacc as bacc
    from concourse.bass_utils import run_bass_kernel_spmd as run

    def arr(name):
        return np.asarray(inputs[name])

    x = arr("x")
    B, N, D = x.shape
    E, H, _ = arr("L0_ffn_w1").shape
    P_, KD, KH = 128, D // 128, H // 128

    def up_T(w):
        return w.reshape(H, KD, P_).transpose(2, 1, 0).reshape(P_, KD * H)

    def down_T(w):
        return w.reshape(D, KH, P_).transpose(2, 1, 0).reshape(P_, KH * D)

    w1, w2 = arr("L0_ffn_w1"), arr("L0_ffn_w2")
    arrays = {
        "in_x": x.reshape(B * N, D),
        "in_adj": arr("adj").reshape(B * N, N),
        "in_W": arr("L0_gnn_W"),
        "in_a": arr("L0_gnn_a"),
        "in_gate_wT": arr("L0_ffn_gate_w").reshape(E, KD, P_).transpose(2, 1, 0),
        "in_experts": np.stack([np.concatenate([up_T(w1[e]), down_T(w2[e])], axis=1) for e in range(E)], axis=1),
        "in_shared": np.concatenate([up_T(arr("L0_ffn_sg_gate")), up_T(arr("L0_ffn_sg_up")), down_T(arr("L0_ffn_sg_down"))], axis=1),
    }
    arrays = {n: np.ascontiguousarray(v) for n, v in arrays.items()}
    nc = bacc.Bacc("TRN2", target_bir_lowering=False, num_devices=1)
    aps = [nc.dram_tensor(n, v.shape, mybir.dt.from_np(v.dtype), kind="ExternalInput").ap() for n, v in arrays.items()]
    out = nc.dram_tensor("out_rows", [B * N, D], F32, kind="ExternalOutput").ap()
    gat_moe(nc, *aps, out)
    r = run(nc, [arrays], core_ids=[0])
    return np.asarray(r.results[0]["out_rows"]).reshape(B, N, D)
```

```python
from contextlib import ExitStack

import concourse.bass as bass
from concourse import mybir

ALU = mybir.AluOpType
ACT = mybir.ActivationFunctionType
AX = mybir.AxisListType
F32 = mybir.dt.float32
F32R = mybir.dt.float32r
BF16 = mybir.dt.bfloat16
I32 = mybir.dt.int32
U32 = mybir.dt.uint32

P = 128
EPS = 1e-5
SLOPE = 0.2
MASK = -1e30


def inside(n, count):
    return not isinstance(n, int) or 0 <= n < count


def through(g, par, each):
    return (g + (2 - par)) * each


def hold(eng, sem):
    eng.sem_inc(sem, 1)


class Chain:

    def __init__(self, eng, sem, done):
        self.eng, self.sem, self.value = eng, sem, done

    def step(self, ins):
        ins.then_inc(self.sem, 1)
        self.value = self.value + 1

    def wait(self):
        self.eng.wait_ge(self.sem, self.value)


def wait_if(eng, sem, value):
    if not isinstance(value, int) or value > 0:
        eng.wait_ge(sem, value)


def gat_moe(nc, x, adj, W, a, gate_wT, experts, shared, out):
    T, D = x.shape
    N = adj.shape[1]
    E = gate_wT.shape[2]
    KD = D // P
    GT = 4
    TG = GT * P
    NG = T // TG
    H = 512
    KH = H // P
    WC = KD * H
    REG = T + P
    NB = 2 * T // P + E
    ST_L, ST_OH, ST_POS, ST = 0, GT * E, 3 * GT * E, 3 * GT * E + 2 * GT

    regions = nc.dram_tensor("regions", [E * REG, D], F32, kind="Internal").ap()
    x2_dram = nc.dram_tensor("x2_rows", [T, D], F32, kind="Internal").ap()
    xT_dram = nc.dram_tensor("xn2_cols", [P, NG, KD, TG], F32, kind="Internal").ap()
    y_dram = nc.dram_tensor("expert_rows", [NB * P, D], F32, kind="Internal").ap()

    with ExitStack() as top:
        def sem(name):
            return top.enter_context(nc.semaphore(name))

        def keep(name, shape, dt=F32):
            return top.enter_context(nc.sbuf_tensor(name, shape, dt))

        w_raw = keep("w_raw", [P, 2, 2 * WC])
        w_first = (sem("w_first_even"), sem("w_first_odd"))
        ident = keep("ident", [P, P])
        stash_all = keep("stash_all", [P, NG, ST])
        tile_row = keep("tile_row", [P, NB], I32)
        tile_exp = keep("tile_exp", [P, NB], I32)
        offset = keep("offset", [P, E])
        gap = keep("gap", [P, NG, GT])
        tile_num = keep("tile_num", [P, NB], I32)
        row_of = keep("row_of", [P, NG, 2 * GT], U32)
        weight_of = keep("weight_of", [P, NG, 2 * GT])

        part_a(nc, top, sem, locals())
        part_b(nc, top, sem, locals())
        part_c(nc, top, sem, locals())


def part_a(nc, top, sem, v):
    x, adj, W, a, gate_wT = v["x"], v["adj"], v["W"], v["a"], v["gate_wT"]
    T, D, N, E, KD, GT, TG, NG = (v[k] for k in ("T", "D", "N", "E", "KD", "GT", "TG", "NG"))
    REG, NB, WC = v["REG"], v["NB"], v["WC"]
    ST_L, ST_OH, ST_POS, ST = v["ST_L"], v["ST_OH"], v["ST_POS"], v["ST"]
    ident, stash_all, tile_row, tile_exp = v["ident"], v["stash_all"], v["tile_row"], v["tile_exp"]
    tile_num, row_of, weight_of = v["tile_num"], v["row_of"], v["weight_of"]
    w_raw, w_first, experts, offset = v["w_raw"], v["w_first"], v["experts"], v["offset"]
    regions, x2_dram, xT_dram = v["regions"], v["x2_dram"], v["xT_dram"]
    WX = D + 2

    with ExitStack() as ctx:
        def sb(name, shape, dt=F32):
            return ctx.enter_context(nc.sbuf_tensor(name, shape, dt))

        def psum(name, shape):
            return ctx.enter_context(nc.psum_tensor(name, shape, F32))

        same_graph = sb("same_graph", [P, P])
        node_of = sb("node_of", [P, N])
        before_f = sb("before_f", [P, P])
        before = sb("before", [P, P], BF16)
        ones_b = sb("ones_b", [P, P], BF16)
        lower_e = sb("lower_e", [P, E, E])
        exp_base_i = sb("exp_base_i", [P, E], I32)
        exp_base = sb("exp_base", [P, E])
        half = sb("half", [P, GT])
        lane_i = sb("lane_i", [P, 1], I32)
        lane = sb("lane", [P, 1])
        jrow_i = sb("jrow_i", [P, NB], I32)
        jrow = sb("jrow", [P, NB])
        jrow128 = sb("jrow128", [P, NB])
        zero_rows = sb("zero_rows", [P, D])
        w_ext = sb("w_ext", [P, KD, WX])
        a_rows = sb("a_rows", [P, 2, D])
        wa_tmp = sb("wa_tmp", [P, D])
        gw = sb("gw", [P, KD, E])
        x_sb = sb("x_sb", [P, 2, GT, D])
        x_again = sb("x_again", [P, 2, GT, D])
        adj_sb = sb("adj_sb", [P, 2, GT, N], I32)
        stats1 = sb("stats1", [P, GT, 6])
        stats2 = sb("stats2", [P, GT, 6])
        mv1 = sb("mv1", [P, 2, GT, 2])
        mv2 = sb("mv2", [P, 2, GT, 2])
        var_eps1 = sb("var_eps1", [P, GT])
        var_eps2 = sb("var_eps2", [P, GT])
        rstd1 = sb("rstd1", [P, 2, GT])
        rstd2 = sb("rstd2", [P, 2, GT])
        shift1 = sb("shift1", [P, 2, GT])
        shift2 = sb("shift2", [P, 2, GT])
        prod1 = sb("prod1", [P, GT])
        prod2 = sb("prod2", [P, GT])
        xn = sb("xn", [P, GT, D])
        xnT = sb("xnT", [P, KD, TG])
        wh = sb("wh", [P, 2, GT, WX])
        ej_diag = sb("ej_diag", [P, GT, N])
        score = sb("score", [P, GT, N])
        leaky = sb("leaky", [P, GT, N])
        mask = sb("mask", [P, GT, N])
        masked = sb("masked", [P, GT, N])
        centred = sb("centred", [P, GT, N])
        row_max = sb("row_max", [P, GT])
        row_sum = sb("row_sum", [P, GT])
        row_inv = sb("row_inv", [P, GT])
        probs = sb("probs", [P, GT, N])
        block_probs = sb("block_probs", [P, GT, P])
        probsT = sb("probsT", [P, GT, P])
        exp_z = sb("exp_z", [P, 2, 2 * D])
        relu_x = sb("relu_x", [P, 2, 2 * D])
        x2 = sb("x2", [P, 2, GT, D])
        xn2 = sb("xn2", [P, 2, GT, D])
        xn2T = sb("xn2T", [P, 2, KD, TG])
        gt = sb("gt", [P, GT, E, E])
        ge = sb("ge", [P, GT, E, E])
        rank = sb("rank", [P, GT, E])
        chosen = sb("chosen", [P, GT * E], BF16)
        stash = sb("stash", [P, ST])
        pos_e = sb("pos_e", [P, GT * E])
        pos_tmp = sb("pos_tmp", [P, 2, GT * E])
        free_row = sb("free_row", [P, E])
        scatter_row = sb("scatter_row", [P, 2, 2 * GT], U32)
        count = sb("count", [P, E])
        count_i = sb("count_i", [P, E], I32)
        tiles_i = sb("tiles_i", [P, E], I32)
        tiles = sb("tiles", [P, E])
        sums = sb("sums", [P, 4, E])
        first_tile = sb("first_tile", [P, E])
        offset_step = sb("offset_step", [P, E])
        pad_f = sb("pad_f", [P, E])
        pad_row = sb("pad_row", [P, E], U32)
        big = [sb(f"big{i}", [P, NB * E]) for i in range(2)]
        tab = sb("tab", [P, 4, NB])

        ps_T = psum("ps_T", [P, KD, TG])
        ps_W = psum("ps_W", [P, 2, 512])
        ps_E = psum("ps_E", [P, 512])
        ps_P = psum("ps_P", [P, GT, P])
        ps_Z = psum("ps_Z", [P, 2, 2 * D])
        E_SC = ps_P[:].rearrange("p t i -> p (t i)")[:, 0:GT * N]
        E_L, E_R, E_TOT = (ps_E[:, n * GT * E:(n + 1) * GT * E] for n in range(3))
        E_TOT = E_TOT[:, 0:E]

        names = ("a_const a_const2 a_wload a_wext mv1_ready ln1_ready xn_ready xnT_ready xnT_copied wh_ready "
                 "wh_copied diag_ready score_ready score_read centred_ready exp_ready probs_ready probsT_ready "
                 "probsT_copied z_ready expz_ready relu_ready x2_ready mv2_ready ln2_ready "
                 "xn2_ready xn2T_ready xn2T_copied logits_ready chosen_ready prefix_ready "
                 "rows_ready pad_ready padded "
                 "c_stats1 c_softmax c_probs c_elu c_rank c_pos c_mid c_ln1 c_ln2 c_setup c_psetup dve_held pool_held")
        S = {n: sem(n) for n in names.split()}
        for n in "a_xin a_again a_adjin x2_stored xT_stored scattered".split():
            S[n] = [sem(n + "_even"), sem(n + "_odd")]
        x_g = x.rearrange("(g t p) d -> p g t d", p=P, t=GT)
        adj_g = adj.rearrange("(g t p) j -> p g t j", p=P, t=GT)
        x2_g = x2_dram.rearrange("(g t p) d -> p g t d", p=P, t=GT)

        def one(ap, g):
            return ap[:, g] if isinstance(g, int) else ap[:, bass.ds(g, 1)].rearrange("p o t d -> p (o t) d")

        block = ctx.enter_context(nc.Block())

        def rounds(eng, body):
            for i in range(-3, 4):
                body(i, i % 2)
            with eng.Fori(0, (NG - 8) // 2) as n:
                for u in range(2):
                    body(n * 2 + (4 + u), u)
            for i in range(NG - 4, NG + 2):
                body(i, i % 2)

        @block.sync
        def _(sp):
            sp.dma_start(w_ext[:, :, 0:D], W.rearrange("(k p) f -> p k f", p=P)).then_inc(S["a_wload"], 16)
            sp.dma_start(a_rows[:], a.rearrange("(o s f) u -> o s (f u)", o=1, s=2).to_broadcast([P, 2, D])).then_inc(S["a_wload"], 16)
            for g in range(2):
                sp.dma_start(x_sb[:, g], one(x_g, g)).then_inc(S["a_xin"][g], 32)
            sp.dma_start(gw[:], gate_wT).then_inc(S["a_wload"], 16)
            for g in range(2):
                sp.dma_start(adj_sb[:, g], one(adj_g, g)).then_inc(S["a_adjin"][g], 32)
                sp.dma_start(x_again[:, g], one(x_g, g)).then_inc(S["a_again"][g], 32)

            def body(i, par):
                if inside(i + 4, NG) and inside(i + 2, NG):
                    sp.wait_ge(S["xn_ready"], i + 3)
                    sp.dma_start(x_sb[:, par], one(x_g, i + 4)).then_inc(S["a_xin"][par], 32)
                if inside(i + 3, NG) and inside(i + 1, NG):
                    sp.wait_ge(S["centred_ready"], i + 2)
                    sp.dma_start(adj_sb[:, 1 - par], one(adj_g, i + 3)).then_inc(S["a_adjin"][1 - par], 32)
                if inside(i - 1, NG):
                    sp.wait_ge(S["xn2T_copied"], i)
                    sp.dma_start(one(xT_dram, i - 1), xn2T[:, 1 - par]).then_inc(S["xT_stored"][1 - par], 32)
                if inside(i, NG):
                    sp.wait_ge(S["mv2_ready"], i + 1)
                    sp.dma_start(one(x2_g, i), x2[:, par]).then_inc(S["x2_stored"][par], 32)
                if inside(i + 2, NG) and inside(i, NG):
                    sp.dma_start(x_again[:, par], one(x_g, i + 2)).then_inc(S["a_again"][par], 32)

            rounds(sp, body)
            for e in range(2):
                sp.dma_start(w_raw[:, e], experts[:, e]).then_inc(w_first[e], 16)
            for par in range(2):
                sp.wait_ge(S["x2_stored"][par], through(NG - 2 + par, par, 16))
                sp.wait_ge(S["xT_stored"][par], through(NG - 2 + par, par, 16))

        @block.gpsimd
        def _(pool):
            ch = Chain(pool, S["c_psetup"], 0)
            ch.step(pool.memset(ident[:], 0.0))
            ch.step(pool.memset(node_of[:], 0.0))
            ch.step(pool.memset(before_f[:], 1.0))
            ch.step(pool.memset(lower_e[:], 1.0))
            ch.step(pool.memset(half[:], -0.5))
            ch.step(pool.memset(zero_rows[:], 0.0))
            ch.step(pool.memset(block_probs[:], 0.0))
            ch.step(pool.memset(ones_b[:], 1.0))
            ch.step(pool.iota(exp_base_i[:], pattern=[[REG, E]], base=0, channel_multiplier=0))
            ch.step(pool.iota(lane_i[:], pattern=[[1, 1]], base=0, channel_multiplier=1))
            ch.step(pool.iota(jrow_i[:], pattern=[[1, NB]], base=0, channel_multiplier=0))
            ch.wait()
            ch.step(pool.affine_select(out=ident[:], in_=ident[:], compare_op=ALU.not_equal, fill=1.0, base=0,
                                       pattern=[[-1, P]], channel_multiplier=1))
            ch.step(pool.affine_select(out=node_of[:], in_=node_of[:], compare_op=ALU.not_equal, fill=1.0, base=0,
                                       pattern=[[-1, N]], channel_multiplier=1))
            ch.step(pool.affine_select(out=before_f[:], in_=before_f[:], compare_op=ALU.is_gt, fill=0.0, base=0,
                                       pattern=[[1, P]], channel_multiplier=-1))
            ch.step(pool.affine_select(out=lower_e[:], in_=lower_e[:], compare_op=ALU.is_gt, fill=0.0, base=0,
                                       pattern=[[1, E], [-1, E]], channel_multiplier=0))
            ch.wait()
            ch.step(pool.affine_select(out=node_of[:], in_=node_of[:], compare_op=ALU.not_equal, fill=1.0, base=-N,
                                       pattern=[[-1, N]], channel_multiplier=1))
            ch.wait()
            pool.tensor_copy(before[:], before_f[:]).then_inc(S["a_const"], 1)

            def layer_norm(g, par, mv, var_eps, rstd, prod, shift, c, ready, used, mv_ready):
                ch = Chain(pool, S[c], g * 3)
                pool.wait_ge(S[mv_ready], g + 1)
                wait_if(pool, S[used], g - 1)
                hold(pool, S["pool_held"])
                ch.step(pool.tensor_scalar(var_eps[:], mv[:, par, :, 1], EPS, None, ALU.add))
                ch.wait()
                ch.step(pool.tensor_tensor(rstd[:, par], var_eps[:], half[:], ALU.pow))
                ch.wait()
                ch.step(pool.tensor_tensor(prod[:], mv[:, par, :, 0], rstd[:, par], ALU.mult))
                ch.wait()
                hold(pool, S["pool_held"])
                pool.tensor_scalar(shift[:, par], prod[:], -1.0, None, ALU.mult).then_inc(S[ready], 1)

            def body(i, par):
                if inside(i - 2, NG):
                    pool.wait_ge(S["rows_ready"], i - 1)
                    hold(pool, S["pool_held"])
                    for s in range(2):
                        for t in range(GT):
                            c = s * GT + t
                            pool.indirect_dma_start(
                                out=regions, out_offset=bass.IndirectOffsetOnAxis(ap=scatter_row[:, par, c:c + 1], axis=0),
                                in_=xn2[:, par, t, :], in_offset=None).then_inc(S["scattered"][par], 32)
                if inside(i, NG):
                    layer_norm(i, par, mv2, var_eps2, rstd2, prod2, shift2, "c_ln2", "ln2_ready", "xn2_ready", "mv2_ready")
                if inside(i + 3, NG):
                    layer_norm(i + 3, 1 - par, mv1, var_eps1, rstd1, prod1, shift1, "c_ln1", "ln1_ready", "xn_ready", "mv1_ready")

            rounds(pool, body)
            pool.wait_ge(S["pad_ready"], 1)
            for e in range(E):
                pool.indirect_dma_start(
                    out=regions, out_offset=bass.IndirectOffsetOnAxis(ap=pad_row[:, e:e + 1], axis=0),
                    in_=zero_rows[:], in_offset=None).then_inc(S["padded"], 16)
            pool.wait_ge(S["padded"], 16 * E)
            for par in range(2):
                pool.wait_ge(S["scattered"][par], through(NG - 2 + par, par, 16 * 2 * GT))

        @block.scalar
        def _(act):
            def normed(g, par, dst, src, rstd, shift, ln_ready, ready):
                act.wait_ge(S[ln_ready], g + 1)
                for t in range(GT):
                    last = act.activation(dst[:, t], src[:, par, t], ACT.Identity,
                                          bias=shift[:, par, t:t + 1], scale=rstd[:, par, t:t + 1])
                last.then_inc(S[ready], 1)

            def body(i, par):
                X, Y, V, Q = i + 2, i + 1, i, i - 1
                hasX, hasY, hasV, hasQ = (inside(g, NG) for g in (X, Y, V, Q))
                if hasQ:
                    wait_if(act, S["xn2T_ready"], Q - 1)
                    wait_if(act, S["scattered"][1 - par], through(Q - 2, 1 - par, 16 * 2 * GT))
                    normed(Q, 1 - par, xn2[:, 1 - par], x2, rstd2, shift2, "ln2_ready", "xn2_ready")
                if hasV:
                    for h in range(2):
                        act.wait_ge(S["z_ready"], V * 2 + (h + 1))
                        wait_if(act, S["x2_ready"], (V - 1) * 2 + (h + 1))
                        act.activation(exp_z[:, h], ps_Z[:, h], ACT.Exp).then_inc(S["expz_ready"], 1)
                if hasX:
                    wait_if(act, S["xnT_ready"], X)
                    normed(X, par, xn, x_sb, rstd1, shift1, "ln1_ready", "xn_ready")
                if hasQ:
                    act.wait_ge(S["xn2T_ready"], Q + 1)
                    wait_if(act, S["logits_ready"], Q - 1)
                    wait_if(act, S["xT_stored"][1 - par], through(Q - 2, 1 - par, 16))
                    for k in range(KD):
                        last = act.copy(xn2T[:, 1 - par, k], ps_T[:, k])
                    last.then_inc(S["xn2T_copied"], 1)
                if hasY:
                    act.wait_ge(S["centred_ready"], Y + 1)
                    act.activation(probs[:], centred[:], ACT.Exp).then_inc(S["exp_ready"], 1)
                if hasX:
                    act.wait_ge(S["xnT_ready"], X + 1)
                    wait_if(act, S["wh_ready"], X * GT)
                    for k in range(KD):
                        last = act.copy(xnT[:, k], ps_T[:, k])
                    last.then_inc(S["xnT_copied"], 1)
                    wait_if(act, S["z_ready"], (X - 1) * 2)
                    for t in range(GT):
                        act.wait_ge(S["wh_ready"], X * GT + (t + 1))
                        act.copy(wh[:, par, t], ps_W[:, t % 2, 0:WX]).then_inc(S["wh_copied"], 1)
                if hasY:
                    act.wait_ge(S["probsT_ready"], Y + 1)
                    wait_if(act, S["z_ready"], Y * 2)
                    act.copy(probsT[:], ps_P[:]).then_inc(S["probsT_copied"], 1)

            rounds(act, body)

        @block.tensor
        def _(pe):
            pe.wait_ge(S["a_const"], 1)
            pe.wait_ge(S["a_wext"], 1)

            def body(i, par):
                X, Y, V, Q, Z = i + 2, i + 1, i, i - 1, i - 2
                hasX, hasY, hasV, hasQ, hasZ = (inside(g, NG) for g in (X, Y, V, Q, Z))
                if hasY:
                    pe.wait_ge(S["diag_ready"], Y + 1)
                    wait_if(pe, S["probsT_copied"], Y)
                    pe.matmul(E_SC, same_graph[:], ej_diag[:].rearrange("p t j -> p (t j)"),
                              start=True, stop=True).then_inc(S["score_ready"], 1)
                if hasV:
                    pe.wait_ge(S["probsT_copied"], V + 1)
                    for t in range(GT):
                        if t % 2 == 0:
                            wait_if(pe, S["relu_ready"], (V - 1) * 2 + (t // 2 + 1))
                        last = pe.matmul(ps_Z[:, t // 2, (t % 2) * D:(t % 2 + 1) * D], probsT[:, t], wh[:, par, t, 0:D],
                                         start=True, stop=True)
                        if t % 2 == 1:
                            last.then_inc(S["z_ready"], 1)
                if hasQ:
                    pe.wait_ge(S["xn2_ready"], Q + 1)
                    pe.wait_ge(S["xnT_copied"], min(Q + 3, NG) if isinstance(Q, int) else Q + 3)
                    for k in range(KD):
                        for t in range(GT):
                            last = pe.transpose(ps_T[:, k, t * P:(t + 1) * P], xn2[:, 1 - par, t, k * P:(k + 1) * P], ident[:])
                    last.then_inc(S["xn2T_ready"], 1)
                if hasZ:
                    pe.wait_ge(S["chosen_ready"], Z + 1)
                    pe.matmul(E_R, before[:], chosen[:], start=True, stop=False)
                    for t in range(1, GT):
                        pe.matmul(E_R[:, t * E:], ones_b[:], chosen[:, 0:(GT - t) * E], start=False, stop=(t == GT - 1))
                    for t in range(GT):
                        last = pe.matmul(E_TOT, ones_b[:], chosen[:, t * E:(t + 1) * E], start=(t == 0), stop=(t == GT - 1))
                    last.then_inc(S["prefix_ready"], 1)
                if hasX:
                    pe.wait_ge(S["xn_ready"], X + 1)
                    wait_if(pe, S["xn2T_copied"], X - 2)
                    for k in range(KD):
                        for t in range(GT):
                            last = pe.transpose(ps_T[:, k, t * P:(t + 1) * P], xn[:, t, k * P:(k + 1) * P], ident[:])
                    last.then_inc(S["xnT_ready"], 1)
                if hasQ:
                    pe.wait_ge(S["xn2T_copied"], Q + 1)
                    wait_if(pe, S["rows_ready"], Q)
                    for t in range(GT):
                        for k in range(KD):
                            last = pe.matmul(E_L[:, t * E:(t + 1) * E], xn2T[:, 1 - par, k, t * P:(t + 1) * P], gw[:, k],
                                             start=(k == 0), stop=(k == KD - 1))
                    last.then_inc(S["logits_ready"], 1)
                if hasX:
                    pe.wait_ge(S["xnT_copied"], X + 1)
                    for t in range(GT):
                        wait_if(pe, S["wh_copied"], X * GT + (t - 1))
                        for k in range(KD):
                            last = pe.matmul(ps_W[:, t % 2, 0:WX], xnT[:, k, t * P:(t + 1) * P], w_ext[:, k],
                                             start=(k == 0), stop=(k == KD - 1))
                        last.then_inc(S["wh_ready"], 1)
                if hasY:
                    pe.wait_ge(S["probs_ready"], Y + 1)
                    for t in range(GT):
                        last = pe.transpose(ps_P[:, t], block_probs[:, t], ident[:])
                    last.then_inc(S["probsT_ready"], 1)

            rounds(pe, body)

        @block.vector
        def _(dve):
            ch = Chain(dve, S["c_setup"], 0)
            ch.step(dve.memset(same_graph[:], 0.0))
            ch.wait()
            ch.step(dve.memset(same_graph[0:N, 0:N], 1.0))
            ch.step(dve.memset(same_graph[N:P, N:P], 1.0))
            dve.wait_ge(S["a_wload"], 48)
            for k in range(KD):
                for s in range(2):
                    ch.step(dve.tensor_tensor_reduce(wa_tmp[:], w_ext[:, k, 0:D], a_rows[:, s], 1.0, 0.0, ALU.mult, ALU.add,
                                                     w_ext[:, k, D + s:D + s + 1]))
                    ch.wait()
            dve.wait_ge(S["a_const"], 1)
            ch.step(dve.tensor_copy(exp_base[:], exp_base_i[:]))
            ch.step(dve.tensor_copy(free_row[:], exp_base_i[:]))
            ch.step(dve.tensor_copy(lane[:], lane_i[:]))
            ch.step(dve.tensor_copy(jrow[:], jrow_i[:]))
            ch.wait()
            ch.step(dve.tensor_scalar(jrow128[:], jrow[:], float(P), None, ALU.mult))
            ch.wait()
            dve.memset(wa_tmp[:, 0:1], 0.0).then_inc(S["a_wext"], 1)

            def spread(ap, n):
                return ap.unsqueeze(2).to_broadcast([P, GT, n])

            def stats(g, par):
                ch = Chain(dve, S["c_stats1"], g * GT)
                wait_if(dve, S["mv1_ready"], g)
                dve.wait_ge(S["a_xin"][par], through(g, par, 16))
                for t in range(GT):
                    ch.step(dve.bn_stats(stats1[:, t], x_sb[:, par, t]))
                ch.wait()
                wait_if(dve, S["ln1_ready"], g - 1)
                hold(dve, S["dve_held"])
                for t in range(GT):
                    last = dve.bn_aggr(mv1[:, par, t], stats1[:, t])
                last.then_inc(S["mv1_ready"], 1)

            def diag(g, par):
                dve.wait_ge(S["wh_copied"], (g + 1) * GT)
                dve.tensor_tensor(ej_diag[:], node_of[:].unsqueeze(1).to_broadcast([P, GT, N]),
                                  wh[:, par, :, D + 1:D + 2].to_broadcast([P, GT, N]), ALU.mult).then_inc(S["diag_ready"], 1)

            def softmax_in(g, par):
                ch = Chain(dve, S["c_softmax"], g * 4)
                dve.wait_ge(S["a_adjin"][par], through(g, par, 16))
                ch.step(dve.tensor_scalar(mask[:], adj_sb[:, par], 0.0, MASK, ALU.is_equal, ALU.mult))
                dve.wait_ge(S["score_ready"], g + 1)
                dve.tensor_tensor(score[:], E_SC.rearrange("p (t j) -> p t j", t=GT),
                                  wh[:, par, :, D:D + 1].to_broadcast([P, GT, N]), ALU.add).then_inc(S["score_read"], 1)
                dve.wait_ge(S["score_read"], g + 1)
                ch.step(dve.scalar_tensor_tensor(out=leaky[:], in0=score[:], scalar=SLOPE, in1=score[:], op0=ALU.mult, op1=ALU.max))
                ch.wait()
                ch.step(dve.tensor_tensor(masked[:], leaky[:], mask[:], ALU.add))
                ch.wait()
                ch.step(dve.tensor_reduce(row_max[:], masked[:], AX.X, ALU.max))
                ch.wait()
                dve.tensor_tensor(centred[:], masked[:], spread(row_max[:], N), ALU.subtract).then_inc(S["centred_ready"], 1)

            def softmax_out(g):
                ch = Chain(dve, S["c_probs"], g * 2)
                dve.wait_ge(S["exp_ready"], g + 1)
                ch.step(dve.tensor_reduce(row_sum[:], probs[:], AX.X, ALU.add))
                ch.wait()
                ch.step(dve.reciprocal(row_inv[:], row_sum[:]))
                ch.wait()
                wait_if(dve, S["probsT_ready"], g)
                for h in range(2):
                    r = slice(h * N, (h + 1) * N)
                    last = dve.tensor_tensor(block_probs[r, :, h * N:(h + 1) * N], probs[r],
                                             row_inv[r].unsqueeze(2).to_broadcast([N, GT, N]), ALU.mult)
                last.then_inc(S["probs_ready"], 1)

            def elu_add(g, par):
                ch = Chain(dve, S["c_elu"], g * GT)
                dve.wait_ge(S["a_again"][par], through(g, par, 16))
                wait_if(dve, S["xn2_ready"], g - 1)
                wait_if(dve, S["x2_stored"][par], through(g - 2, par, 16))
                for h in range(2):
                    ts = slice(2 * h, 2 * h + 2)
                    dve.wait_ge(S["expz_ready"], g * 2 + (h + 1))
                    dve.scalar_tensor_tensor(out=relu_x[:, h], in0=ps_Z[:, h], scalar=0.0,
                                             in1=x_again[:, par, ts].rearrange("p t d -> p (t d)"),
                                             op0=ALU.max, op1=ALU.add).then_inc(S["relu_ready"], 1)
                    dve.wait_ge(S["relu_ready"], g * 2 + (h + 1))
                    dve.scalar_tensor_tensor(out=x2[:, par, ts].rearrange("p t d -> p (t d)"), in0=exp_z[:, h], scalar=1.0,
                                             in1=relu_x[:, h], op0=ALU.min, op1=ALU.add).then_inc(S["x2_ready"], 1)
                    dve.wait_ge(S["x2_ready"], g * 2 + (h + 1))
                    for t in range(2 * h, 2 * h + 2):
                        ch.step(dve.bn_stats(stats2[:, t], x2[:, par, t]))
                ch.wait()
                wait_if(dve, S["ln2_ready"], g - 1)
                hold(dve, S["dve_held"])
                for t in range(GT):
                    last = dve.bn_aggr(mv2[:, par, t], stats2[:, t])
                last.then_inc(S["mv2_ready"], 1)

            def choose(g):
                ch = Chain(dve, S["c_rank"], g * 8)
                dve.wait_ge(S["logits_ready"], g + 1)
                L = stash[:, ST_L:ST_L + GT * E].rearrange("p (t e) -> p t e", t=GT)
                ch.step(dve.tensor_copy(stash[:, ST_L:ST_L + GT * E], E_L))
                ch.wait()
                other = L.unsqueeze(2).to_broadcast([P, GT, E, E])
                own = L.unsqueeze(3).to_broadcast([P, GT, E, E])
                ch.step(dve.tensor_tensor(gt[:], other, own, ALU.is_gt))
                ch.step(dve.tensor_tensor(ge[:], other, own, ALU.is_ge))
                ch.wait()
                ch.step(dve.tensor_tensor(ge[:], ge[:], lower_e[:].unsqueeze(1).to_broadcast([P, GT, E, E]), ALU.mult))
                ch.wait()
                ch.step(dve.tensor_tensor(gt[:], gt[:], ge[:], ALU.max))
                ch.wait()
                ch.step(dve.tensor_reduce(rank[:], gt[:], AX.X, ALU.add))
                ch.wait()
                R = rank[:].rearrange("p t e -> p (t e)")
                dve.tensor_scalar(chosen[:], R, 2.0, None, ALU.is_lt).then_inc(S["chosen_ready"], 1)
                for s in range(2):
                    ch.step(dve.tensor_scalar(stash[:, ST_OH + s * GT * E:ST_OH + (s + 1) * GT * E], R, float(s), None, ALU.is_equal))

            def place(g, par):
                ch = Chain(dve, S["c_pos"], g * 5)
                dve.wait_ge(S["c_rank"], (g + 1) * 8)
                dve.wait_ge(S["prefix_ready"], g + 1)
                ch.step(dve.tensor_tensor(pos_e[:].rearrange("p (t e) -> p t e", t=GT), E_R.rearrange("p (t e) -> p t e", t=GT),
                                          free_row[:].unsqueeze(1).to_broadcast([P, GT, E]), ALU.add))
                ch.wait()
                ch.step(dve.tensor_tensor(free_row[:], free_row[:], E_TOT, ALU.add))
                ch.step(dve.tensor_tensor(pos_tmp[:], stash[:, ST_OH:ST_POS].rearrange("p (s c) -> p s c", s=2),
                                          pos_e[:].unsqueeze(1).to_broadcast([P, 2, GT * E]), ALU.mult))
                ch.wait()
                ch.step(dve.tensor_reduce(stash[:, ST_POS:ST], pos_tmp[:].rearrange("p s (t e) -> p (s t) e", e=E), AX.X, ALU.add))
                ch.wait()
                wait_if(dve, S["scattered"][par], through(g - 2, par, 16 * 2 * GT))
                dve.tensor_copy(scatter_row[:, par], stash[:, ST_POS:ST]).then_inc(S["rows_ready"], 1)
                if isinstance(g, int):
                    dst = stash_all[:, g]
                else:
                    dst = stash_all[:, bass.ds(g, 1)].rearrange("p o c -> p (o c)")
                ch.step(dve.tensor_copy(dst, stash[:]))
                ch.wait()

            def body(i, par):
                U, Y, V, Z = i + 3, i + 1, i, i - 2
                hasU, hasY, hasV, hasZ = (inside(g, NG) for g in (U, Y, V, Z))
                if hasY:
                    diag(Y, 1 - par)
                if hasU:
                    stats(U, 1 - par)
                if hasZ:
                    choose(Z)
                    place(Z, par)
                if hasY:
                    softmax_in(Y, 1 - par)
                if hasV:
                    elu_add(V, par)
                if hasY:
                    softmax_out(Y)

            rounds(dve, body)

            ch = Chain(dve, S["c_mid"], 0)

            def do(ins):
                ch.step(ins)
                ch.wait()

            do(dve.tensor_tensor(count[:], free_row[:], exp_base[:], ALU.subtract))
            do(dve.tensor_scalar(pad_f[:], free_row[:], lane[:, 0:1], None, ALU.add))
            dve.tensor_copy(pad_row[:], pad_f[:]).then_inc(S["pad_ready"], 1)
            do(dve.tensor_scalar(count_i[:], count[:], float(P - 1), None, ALU.add))
            do(dve.tensor_scalar(tiles_i[:], count_i[:], 7, None, ALU.logical_shift_right))
            do(dve.tensor_copy(tiles[:], tiles_i[:]))
            do(dve.tensor_copy(sums[:, 0], tiles_i[:]))
            for n, d in enumerate((1, 2, 4)):
                do(dve.tensor_copy(sums[:, n + 1, 0:d], sums[:, n, 0:d]))
                do(dve.tensor_tensor(sums[:, n + 1, d:E], sums[:, n, d:E], sums[:, n, 0:E - d], ALU.add))
            end_tile = sums[:, 3]
            do(dve.tensor_tensor(first_tile[:], end_tile, tiles[:], ALU.subtract))
            do(dve.scalar_tensor_tensor(out=offset[:], in0=first_tile[:], scalar=-float(P), in1=exp_base[:], op0=ALU.mult, op1=ALU.add))
            b = [t[:].rearrange("p (j e) -> p j e", e=E) for t in big]

            def by_e(ap):
                return ap.unsqueeze(1).to_broadcast([P, NB, E])

            def by_j(ap):
                return ap.unsqueeze(2).to_broadcast([P, NB, E])

            do(dve.tensor_copy(offset_step[:, 0:1], offset[:, 0:1]))
            do(dve.tensor_tensor(offset_step[:, 1:E], offset[:, 1:E], offset[:, 0:E - 1], ALU.subtract))
            do(dve.tensor_tensor(b[0], by_j(jrow[:]), by_e(first_tile[:]), ALU.is_ge))
            ch.step(dve.tensor_reduce(tab[:, 1], b[0], AX.X, ALU.add))
            do(dve.tensor_tensor(b[1], b[0], by_e(offset_step[:]), ALU.mult))
            do(dve.tensor_reduce(tab[:, 0], b[1], AX.X, ALU.add))
            do(dve.tensor_tensor(tab[:, 0], tab[:, 0], jrow128[:], ALU.add))
            do(dve.tensor_scalar(tab[:, 2], jrow[:], end_tile[:, E - 1:E], None, ALU.is_lt))
            do(dve.scalar_tensor_tensor(out=tab[:, 3], in0=tab[:, 0], scalar=-float((E - 1) * REG), in1=tab[:, 2], op0=ALU.add, op1=ALU.mult))
            do(dve.tensor_scalar(tile_row[:], tab[:, 3], float((E - 1) * REG), None, ALU.add))
            do(dve.tensor_scalar(tile_exp[:], tab[:, 1], -1.0, float(2 * WC), ALU.add, ALU.mult))
            do(dve.tensor_copy(tile_num[:], tab[:, 1]))


def part_b(nc, top, sem, v):
    experts, E, D, KD, H, KH, WC, NB = (v[k] for k in ("experts", "E", "D", "KD", "H", "KH", "WC", "NB"))
    ident, tile_row, tile_exp, tile_num, regions, y_dram = (v[k] for k in ("ident", "tile_row", "tile_exp", "tile_num", "regions", "y_dram"))
    REG, NG, GT, stash_all, offset = (v[k] for k in ("REG", "NG", "GT", "stash_all", "offset"))
    ST_L, ST_OH, ST_POS, ST = (v[k] for k in ("ST_L", "ST_OH", "ST_POS", "ST"))
    w_raw, w_first, row_of, gap = (v[k] for k in ("w_raw", "w_first", "row_of", "gap"))
    with ExitStack() as ctx:
        def sb(name, shape, dt=F32):
            return ctx.enter_context(nc.sbuf_tensor(name, shape, dt))

        def psum(name, shape):
            return ctx.enter_context(nc.psum_tensor(name, shape, F32))

        w_hi = sb("w_hi", [P, E * 2 * WC], F32R)
        w_lo = sb("w_lo", [P, E * 2 * WC], F32R)
        rows = sb("rows", [P, 2, D])
        xT_hi = sb("xT_hi", [P, 2, KD, P], F32R)
        xT_lo = sb("xT_lo", [P, 2, KD, P], F32R)
        hid = sb("hid", [P, 2, H])
        hT_hi = sb("hT_hi", [P, 2, KH, P], F32R)
        hT_lo = sb("hT_lo", [P, 2, KH, P], F32R)
        y_sb = sb("y_sb", [P, 2, D])
        picked = sb("picked", [P, NG * 2 * GT * E])
        picked_sum = sb("picked_sum", [P, NG, 2 * GT])
        v_top = sb("v_top", [P, NG, 2, GT])
        ps_X = psum("ps_X", [P, 512])
        ps_H = psum("ps_H", [P, 2, H])
        ps_HT = psum("ps_HT", [P, 2, KH, P])
        ps_Y = psum("ps_Y", [P, 2, 512])

        names = ("w_first_hi w_first_split w_split_hi w_split xT_ready xhi_ready xlo_ready h_ready silu_ready hT_ready "
                 "hhi_ready hlo_ready y_ready y_copied tables")
        S = {n: sem("b_" + n) for n in names.split()}
        for n in "w_loaded rows_loaded y_stored".split():
            S[n] = [sem(f"b_{n}_even"), sem(f"b_{n}_odd")]
        block = ctx.enter_context(nc.Block())

        EARLY = 8

        def steps(eng, body, by_weights=False):
            for j in range(-1, 4):
                body(j, j % 4, *([True] * by_weights))
            if by_weights:
                with eng.Fori(0, EARLY) as n:
                    for u in range(4):
                        body(n * 4 + (4 + u), u, True)
                eng.wait_ge(S["w_split"], E)
                with eng.Fori(EARLY, (NB - 8) // 4) as n:
                    for u in range(4):
                        body(n * 4 + (4 + u), u)
            else:
                with eng.Fori(0, (NB - 8) // 4) as n:
                    for u in range(4):
                        body(n * 4 + (4 + u), u)
            for j in range(NB - 4, NB + 2):
                body(j, j % 4)

        @block.sync
        def _(sp):
            def load(j, par):
                r = sp.value_load(tile_row[0:1, bass.ds(j, 1)], min_val=0, max_val=E * REG - P)
                sp.dma_start(rows[:, par], regions[bass.ds(r, P), :]).then_inc(S["rows_loaded"][par], 32)

            def body(j, slot):
                par = slot % 2
                if inside(j + 2, NB) and (not isinstance(j, int) or j >= 0):
                    sp.wait_ge(S["xT_ready"], j + 1)
                    load(j + 2, par)
                if inside(j - 2, NB):
                    sp.wait_ge(S["y_copied"], j - 1)
                    row = (j - 2) * P
                    dst = y_dram[row:row + P] if isinstance(j, int) else y_dram[bass.ds(row, P)]
                    sp.dma_start(dst, y_sb[:, par]).then_inc(S["y_stored"][par], 32)

            load(0, 0)
            load(1, 1)
            steps(sp, body)
            for par in range(2):
                sp.wait_ge(S["y_stored"][par], through(NB - 2 + par, par, 16))

        @block.gpsimd
        def _(pool):
            pool.wait_ge(w_first[1], 16)
            pool.wait_ge(S["w_first_split"], 1)
            pool.dma_start(w_raw[:, 0], experts[:, 2]).then_inc(S["w_loaded"][0], 16)
            pool.sem_inc(S["w_split"], 1)
            for e in range(1, E):
                c = slice(e * 2 * WC, (e + 1) * 2 * WC)
                if e >= 2:
                    pool.wait_ge(S["w_loaded"][e % 2], 16 * (e // 2))
                pool.tensor_copy(w_hi[:, c], w_raw[:, e % 2]).then_inc(S["w_split_hi"], 1)
                pool.wait_ge(S["w_split_hi"], e)
                pool.tensor_tensor(w_lo[:, c], w_raw[:, e % 2], w_hi[:, c].bitcast(F32), ALU.subtract).then_inc(S["w_split"], 1)
                if e + 2 < E:
                    pool.wait_ge(S["w_split"], e + 1)
                    pool.dma_start(w_raw[:, e % 2], experts[:, e + 2]).then_inc(S["w_loaded"][e % 2], 16)

        @block.scalar
        def _(act):
            def body(j, slot):
                par = slot % 2
                if inside(j, NB):
                    act.wait_ge(S["h_ready"], j + 1)
                    act.activation(hid[:, par], ps_H[:, par], ACT.Silu).then_inc(S["silu_ready"], 1)
                if inside(j + 1, NB):
                    act.wait_ge(S["xT_ready"], j + 2)
                    act.copy(xT_hi[:, 1 - par].rearrange("p k t -> p (k t)"), ps_X[:, 0:D]).then_inc(S["xhi_ready"], 1)
                if inside(j - 1, NB):
                    act.wait_ge(S["hT_ready"], j)
                    wait_if(act, S["y_ready"], j - 2)
                    act.copy(hT_hi[:, 1 - par], ps_HT[:, 1 - par]).then_inc(S["hhi_ready"], 1)

            act.wait_ge(w_first[0], 16)
            act.copy(w_hi[:, 0:2 * WC], w_raw[:, 0]).then_inc(S["w_first_hi"], 1)
            steps(act, body)

        @block.vector
        def _(dve):
            def body(j, slot):
                par = slot % 2
                if inside(j + 1, NB):
                    dve.wait_ge(S["xhi_ready"], j + 2)
                    q = xT_hi[:, 1 - par].rearrange("p k t -> p (k t)")
                    dve.tensor_tensor(xT_lo[:, 1 - par].rearrange("p k t -> p (k t)"), ps_X[:, 0:D], q.bitcast(F32),
                                      ALU.subtract).then_inc(S["xlo_ready"], 1)
                if inside(j - 1, NB):
                    dve.wait_ge(S["hhi_ready"], j)
                    dve.tensor_tensor(hT_lo[:, 1 - par], ps_HT[:, 1 - par], hT_hi[:, 1 - par].bitcast(F32),
                                      ALU.subtract).then_inc(S["hlo_ready"], 1)
                if inside(j - 2, NB):
                    dve.wait_ge(S["y_ready"], j - 1)
                    wait_if(dve, S["y_stored"][par], through(j - 4, par, 16))
                    dve.tensor_copy(y_sb[:, par], ps_Y[:, par, 0:D]).then_inc(S["y_copied"], 1)

            dve.wait_ge(S["w_first_hi"], 1)
            dve.tensor_tensor(w_lo[:, 0:2 * WC], w_raw[:, 0], w_hi[:, 0:2 * WC].bitcast(F32), ALU.subtract).then_inc(S["w_first_split"], 1)
            steps(dve, body)
            ch = Chain(dve, S["tables"], 0)

            def do(ins):
                ch.step(ins)
                ch.wait()

            oh = stash_all[:, :, ST_OH:ST_POS].rearrange("p g (c e) -> p g c e", e=E)
            do(dve.tensor_tensor(picked[:].rearrange("p (g c e) -> p g c e", e=E, g=NG), oh,
                                 offset[:].unsqueeze(1).unsqueeze(1).to_broadcast([P, NG, 2 * GT, E]), ALU.mult))
            do(dve.tensor_reduce(picked_sum[:], picked[:].rearrange("p (g c e) -> p g c e", e=E, g=NG), AX.X, ALU.add))
            do(dve.tensor_tensor(row_of[:], stash_all[:, :, ST_POS:ST], picked_sum[:], ALU.subtract))
            half = picked[:, 0:NG * GT * E]
            for s in range(2):
                do(dve.tensor_tensor(half.rearrange("p (g c) -> p g c", g=NG),
                                     stash_all[:, :, ST_OH + s * GT * E:ST_OH + (s + 1) * GT * E],
                                     stash_all[:, :, ST_L:ST_L + GT * E], ALU.mult))
                do(dve.tensor_reduce(v_top[:, :, s], half.rearrange("p (g t e) -> p g t e", g=NG, e=E), AX.X, ALU.add))
            do(dve.tensor_tensor(gap[:], v_top[:, :, 1], v_top[:, :, 0], ALU.subtract))

        @block.tensor
        def _(pe):
            start_of = [pe.alloc_register(f"weights_{n}") for n in range(4)]

            def start(slot):
                return pe.snap(start_of[slot % 4], min_val=0, max_val=(E - 1) * 2 * WC)

            def body(j, slot, waiting=False):
                par = slot % 2
                if inside(j, NB):
                    base = start(slot)
                if inside(j - 2, NB):
                    base2 = start(slot - 2)
                if inside(j, NB) and waiting:
                    pe.wait_ge(S["w_split"], pe.value_load(tile_num[0:1, bass.ds(j, 1)], min_val=1, max_val=E))
                if inside(j, NB):
                    pe.wait_ge(S["xlo_ready"], j + 1)
                    n = 0
                    for k in range(KD):
                        for lhs, rhs in ((xT_hi, w_hi), (xT_lo, w_hi), (xT_hi, w_lo)):
                            last = pe.matmul(ps_H[:, par], lhs[:, par, k], rhs[:, bass.ds(base + k * H, H)],
                                             start=(n == 0), stop=(n == 3 * KD - 1))
                            n += 1
                    last.then_inc(S["h_ready"], 1)
                if inside(j - 1, NB):
                    pe.wait_ge(S["silu_ready"], j)
                    for k in range(KH):
                        last = pe.transpose(ps_HT[:, 1 - par, k], hid[:, 1 - par, k * P:(k + 1) * P], ident[:])
                    last.then_inc(S["hT_ready"], 1)
                if inside(j + 1, NB):
                    pe.wait_ge(S["rows_loaded"][1 - par], through(j + 1, 1 - par, 16))
                    for k in range(KD):
                        last = pe.transpose(ps_X[:, k * P:(k + 1) * P], rows[:, 1 - par, k * P:(k + 1) * P], ident[:])
                    last.then_inc(S["xT_ready"], 1)
                if inside(j - 2, NB):
                    pe.wait_ge(S["hlo_ready"], j - 1)
                    wait_if(pe, S["y_copied"], j - 3)
                    n = 0
                    for k in range(KH):
                        for lhs, rhs in ((hT_hi, w_hi), (hT_lo, w_hi), (hT_hi, w_lo)):
                            last = pe.matmul(ps_Y[:, par, 0:D], lhs[:, par, k], rhs[:, bass.ds(base2 + (WC + k * D), D)],
                                             start=(n == 0), stop=(n == 3 * KH - 1))
                            n += 1
                    last.then_inc(S["y_ready"], 1)
                if inside(j + 1, NB):
                    pe.reg_load(start_of[(slot + 1) % 4], tile_exp[0:1, bass.ds(j + 1, 1)])

            steps(pe, body, True)


def part_c(nc, top, sem, v):
    shared, D, KD, H, KH, WC, NG, GT, TG = (v[k] for k in ("shared", "D", "KD", "H", "KH", "WC", "NG", "GT", "TG"))
    gap = v["gap"]
    row_of, weight_of, y_dram, x2_dram, xT_dram, out = (v[k] for k in ("row_of", "weight_of", "y_dram", "x2_dram", "xT_dram", "out"))
    with ExitStack() as ctx:
        def sb(name, shape, dt=F32):
            return ctx.enter_context(nc.sbuf_tensor(name, shape, dt))

        def psum(name, shape):
            return ctx.enter_context(nc.psum_tensor(name, shape, F32))

        gap_exp = sb("gap_exp", [P, NG, GT])
        gap_sum = sb("gap_sum", [P, NG, GT])
        gap_inv = sb("gap_inv", [P, NG, GT])
        s_raw = sb("s_raw", [P, 3 * WC])
        s_hi = sb("s_hi", [P, 3, WC], F32R)
        s_lo = sb("s_lo", [P, 3, WC], F32R)
        xT = sb("xT", [P, 2, KD, TG])
        xT_h = sb("xT_h", [P, 2, KD, TG], F32R)
        xT_l = sb("xT_l", [P, 2, KD, TG], F32R)
        x2_in = sb("x2_in", [P, 2, GT, D])
        gate = sb("gate", [P, 2, TG])
        hidT = sb("hidT", [P, 2, TG])
        hidT_h = sb("hidT_h", [P, 2, KH, TG], F32R)
        hidT_l = sb("hidT_l", [P, 2, KH, TG], F32R)
        rows_l = sb("rows_l", [P, 2, 2 * GT], U32)
        weights_l = sb("weights_l", [P, 2, 2 * GT])
        y_in = sb("y_in", [P, 2, 2, GT, D])
        out_sb = sb("out_sb", [P, 2, GT, D])
        ps_G = psum("ps_G", [P, 2, TG])
        ps_U = psum("ps_U", [P, 2, TG])
        ps_D = psum("ps_D", [P, 2, 2, D])

        names = ("s_loaded s_hi_ready s_split xhi_ready xlo_ready gate_ready up_ready silu_ready "
                 "hid_ready hhi_ready hlo_ready down_ready idx_ready first_ready out_ready c_comb held gap_exp_ready weights")
        S = {n: sem("c_" + n) for n in names.split()}
        for n in "xT_loaded x2_loaded gathered stored".split():
            S[n] = [sem(f"c_{n}_even"), sem(f"c_{n}_odd")]
        x2_g = x2_dram.rearrange("(g t p) d -> p g t d", p=P, t=GT)
        out_g = out.rearrange("(g t p) d -> p g t d", p=P, t=GT)

        def one(ap, g):
            return ap[:, g] if isinstance(g, int) else ap[:, bass.ds(g, 1)].rearrange("p o t d -> p (o t) d")

        block = ctx.enter_context(nc.Block())

        def rounds(eng, body):
            for g in range(4):
                body(g, g % 2)
            with eng.Fori(0, (NG - 6) // 2) as n:
                for u in range(2):
                    body(n * 2 + (4 + u), u)
            for g in range(NG - 2, NG + 1):
                body(g, g % 2)

        @block.sync
        def _(sp):
            sp.dma_start(s_raw[:], shared).then_inc(S["s_loaded"], 16)

            def body(g, par):
                if inside(g, NG):
                    wait_if(sp, S["xlo_ready"], g - 1)
                    sp.dma_start(xT[:, par], one(xT_dram, g)).then_inc(S["xT_loaded"][par], 32)
                    wait_if(sp, S["out_ready"], (g - 1) * GT)
                    sp.dma_start(x2_in[:, par], one(x2_g, g)).then_inc(S["x2_loaded"][par], 32)
                if inside(g - 2, NG):
                    sp.wait_ge(S["out_ready"], (g - 1) * GT)
                    sp.dma_start(one(out_g, g - 2), out_sb[:, par]).then_inc(S["stored"][par], 32)

            for g in range(4):
                body(g, g % 2)
            with sp.Fori(0, (NG - 6) // 2) as n:
                for u in range(2):
                    body(n * 2 + (4 + u), u)
            for g in range(NG - 2, NG + 2):
                body(g, g % 2)
            for par in range(2):
                sp.wait_ge(S["stored"][par], through(NG - 2 + par, par, 16))

        @block.gpsimd
        def _(pool):
            def body(g, par):
                if inside(g, NG):
                    pool.wait_ge(S["idx_ready"], g + 1)
                    wait_if(pool, S["out_ready"], (g - 1) * GT)
                    hold(pool, S["held"])
                    for s in range(2):
                        for t in range(GT):
                            c = s * GT + t
                            pool.indirect_dma_start(
                                out=y_in[:, par, s, t], out_offset=None, in_=y_dram,
                                in_offset=bass.IndirectOffsetOnAxis(ap=rows_l[:, par, c:c + 1], axis=0)).then_inc(S["gathered"][par], 32)

            rounds(pool, body)

        @block.scalar
        def _(act):
            act.activation(gap_exp[:], gap[:], ACT.Exp).then_inc(S["gap_exp_ready"], 1)
            act.wait_ge(S["s_loaded"], 16)
            act.copy(s_hi[:].rearrange("p m c -> p (m c)"), s_raw[:]).then_inc(S["s_hi_ready"], 1)

            def split(g, par):
                act.wait_ge(S["xT_loaded"][par], through(g, par, 16))
                wait_if(act, S["up_ready"], (g - 1) * KH)
                act.copy(xT_h[:, par], xT[:, par]).then_inc(S["xhi_ready"], 1)

            split(0, 0)

            def body(g, par):
                if not inside(g, NG):
                    return
                for b in range(KH):
                    act.wait_ge(S["gate_ready"], g * KH + (b + 1))
                    wait_if(act, S["hid_ready"], g * KH + (b - 1))
                    act.activation(gate[:, b % 2], ps_G[:, b % 2], ACT.Silu).then_inc(S["silu_ready"], 1)
                    act.wait_ge(S["hid_ready"], g * KH + (b + 1))
                    if b == 0:
                        wait_if(act, S["down_ready"], (g - 1) * 2)
                    act.copy(hidT_h[:, par, b], hidT[:, b % 2]).then_inc(S["hhi_ready"], 1)
                    if b == 1 and inside(g + 1, NG):
                        split(g + 1, 1 - par)

            rounds(act, body)

        @block.vector
        def _(dve):
            ch = Chain(dve, S["weights"], 0)
            dve.wait_ge(S["gap_exp_ready"], 1)
            ch.step(dve.tensor_scalar(gap_sum[:], gap_exp[:], 1.0, None, ALU.add))
            ch.wait()
            ch.step(dve.reciprocal(gap_inv[:], gap_sum[:]))
            ch.wait()
            ch.step(dve.tensor_copy(weight_of[:, :, 0:GT], gap_inv[:]))
            ch.step(dve.tensor_tensor(weight_of[:, :, GT:2 * GT], gap_exp[:], gap_inv[:], ALU.mult))
            ch.wait()
            dve.wait_ge(S["s_hi_ready"], 1)
            dve.tensor_tensor(s_lo[:].rearrange("p m c -> p (m c)"), s_raw[:], s_hi[:].rearrange("p m c -> p (m c)").bitcast(F32),
                              ALU.subtract).then_inc(S["s_split"], 1)

            def split(g, par):
                dve.wait_ge(S["xhi_ready"], g + 1)
                wait_if(dve, S["up_ready"], (g - 1) * KH)
                dve.tensor_tensor(xT_l[:, par], xT[:, par], xT_h[:, par].bitcast(F32), ALU.subtract).then_inc(S["xlo_ready"], 1)

            split(0, 0)

            def tables(g, par):
                wait_if(dve, S["gathered"][par], through(g - 2, par, 16 * 2 * GT))
                wait_if(dve, S["out_ready"], (g - 1) * GT)
                r, w = (t[:, g] if isinstance(g, int) else t[:, bass.ds(g, 1)].rearrange("p o c -> p (o c)") for t in (row_of, weight_of))
                dve.tensor_copy(rows_l[:, par], r)
                dve.tensor_copy(weights_l[:, par], w).then_inc(S["idx_ready"], 1)

            def combine(g, par, h):
                ch = Chain(dve, S["c_comb"], g * GT + h * 2)
                if h == 0:
                    dve.wait_ge(S["x2_loaded"][par], through(g, par, 16))
                    wait_if(dve, S["stored"][par], through(g - 2, par, 16))
                    dve.wait_ge(S["gathered"][par], through(g, par, 16 * 2 * GT))
                    dve.wait_ge(S["idx_ready"], g + 1)
                ts = slice(2 * h, 2 * h + 2)
                dve.wait_ge(S["down_ready"], g * 2 + (h + 1))
                dve.scalar_tensor_tensor(out=out_sb[:, par, ts], in0=ps_D[:, h], scalar=-1.0, in1=x2_in[:, par, ts],
                                         op0=ALU.add, op1=ALU.add).then_inc(S["first_ready"], 1)
                dve.wait_ge(S["first_ready"], g * 2 + (h + 1))
                for t in range(2 * h, 2 * h + 2):
                    ch.step(dve.scalar_tensor_tensor(out=out_sb[:, par, t], in0=y_in[:, par, 0, t], scalar=weights_l[:, par, t:t + 1],
                                                     in1=out_sb[:, par, t], op0=ALU.mult, op1=ALU.add))
                ch.wait()
                for t in range(2 * h, 2 * h + 2):
                    dve.scalar_tensor_tensor(out=out_sb[:, par, t], in0=y_in[:, par, 1, t], scalar=weights_l[:, par, GT + t:GT + t + 1],
                                             in1=out_sb[:, par, t], op0=ALU.mult, op1=ALU.add).then_inc(S["out_ready"], 1)

            def body(g, par):
                if inside(g, NG):
                    tables(g, par)
                    for b in range(KH):
                        dve.wait_ge(S["silu_ready"], g * KH + (b + 1))
                        dve.wait_ge(S["up_ready"], g * KH + (b + 1))
                        dve.tensor_tensor(hidT[:, b % 2], ps_U[:, b % 2], gate[:, b % 2], ALU.mult).then_inc(S["hid_ready"], 1)
                        dve.wait_ge(S["hhi_ready"], g * KH + (b + 1))
                        dve.tensor_tensor(hidT_l[:, par, b], hidT[:, b % 2], hidT_h[:, par, b].bitcast(F32),
                                          ALU.subtract).then_inc(S["hlo_ready"], 1)
                        if b == 1 and inside(g + 1, NG):
                            split(g + 1, 1 - par)
                        if b == 1 and inside(g - 1, NG):
                            combine(g - 1, 1 - par, 0)
                elif inside(g - 1, NG):
                    combine(g - 1, 1 - par, 0)
                if inside(g - 1, NG):
                    combine(g - 1, 1 - par, 1)

            rounds(dve, body)

        @block.tensor
        def _(pe):
            pe.wait_ge(S["s_split"], 1)

            def up_product(dst, m, par, b):
                n = 0
                for k in range(KD):
                    col = slice(k * H + b * P, k * H + (b + 1) * P)
                    for lhs, rhs in ((s_hi, xT_h), (s_lo, xT_h), (s_hi, xT_l)):
                        last = pe.matmul(dst, lhs[:, m, col], rhs[:, par, k], start=(n == 0), stop=(n == 3 * KD - 1))
                        n += 1
                return last

            def down(G, par, h):
                if h == 0:
                    pe.wait_ge(S["hlo_ready"], (G + 1) * KH)
                wait_if(pe, S["first_ready"], (G - 1) * 2 + (h + 1))
                for t in range(2):
                    n = 0
                    for k in range(KH):
                        col = slice((2 * h + t) * P, (2 * h + t + 1) * P)
                        for lhs, rhs in ((hidT_h, s_hi), (hidT_l, s_hi), (hidT_h, s_lo)):
                            last = pe.matmul(ps_D[:, h, t], lhs[:, par, k, col], rhs[:, 2, k * D:(k + 1) * D],
                                             start=(n == 0), stop=(n == 3 * KH - 1))
                            n += 1
                last.then_inc(S["down_ready"], 1)

            def body(g, par):
                if inside(g, NG):
                    pe.wait_ge(S["xlo_ready"], g + 1)
                for b in range(KH):
                    if inside(g, NG):
                        wait_if(pe, S["silu_ready"], g * KH + (b - 1))
                        up_product(ps_G[:, b % 2], 0, par, b).then_inc(S["gate_ready"], 1)
                        wait_if(pe, S["hid_ready"], g * KH + (b - 1))
                        up_product(ps_U[:, b % 2], 1, par, b).then_inc(S["up_ready"], 1)
                    if b % 2 == 1 and inside(g - 1, NG):
                        down(g - 1, 1 - par, b // 2)

            rounds(pe, body)


def kernel(**inputs):
    import numpy as np
    import concourse.bacc as bacc
    from concourse.bass_utils import run_bass_kernel_spmd as run

    def arr(name):
        return np.asarray(inputs[name])

    x = arr("x")
    B, N, D = x.shape
    E, H, _ = arr("L0_ffn_w1").shape
    P_, KD, KH = 128, D // 128, H // 128

    def up_T(w):
        return w.reshape(H, KD, P_).transpose(2, 1, 0).reshape(P_, KD * H)

    def down_T(w):
        return w.reshape(D, KH, P_).transpose(2, 1, 0).reshape(P_, KH * D)

    w1, w2 = arr("L0_ffn_w1"), arr("L0_ffn_w2")
    arrays = {
        "in_x": x.reshape(B * N, D),
        "in_adj": arr("adj").reshape(B * N, N),
        "in_W": arr("L0_gnn_W"),
        "in_a": arr("L0_gnn_a"),
        "in_gate_wT": arr("L0_ffn_gate_w").reshape(E, KD, P_).transpose(2, 1, 0),
        "in_experts": np.stack([np.concatenate([up_T(w1[e]), down_T(w2[e])], axis=1) for e in range(E)], axis=1),
        "in_shared": np.concatenate([up_T(arr("L0_ffn_sg_gate")), up_T(arr("L0_ffn_sg_up")), down_T(arr("L0_ffn_sg_down"))], axis=1),
    }
    arrays = {n: np.ascontiguousarray(v) for n, v in arrays.items()}
    nc = bacc.Bacc("TRN2", target_bir_lowering=False, num_devices=1)
    aps = [nc.dram_tensor(n, v.shape, mybir.dt.from_np(v.dtype), kind="ExternalInput").ap() for n, v in arrays.items()]
    out = nc.dram_tensor("out_rows", [B * N, D], F32, kind="ExternalOutput").ap()
    gat_moe(nc, *aps, out)
    r = run(nc, [arrays], core_ids=[0])
    return np.asarray(r.results[0]["out_rows"]).reshape(B, N, D)
```

```python
from contextlib import ExitStack

import concourse.bass as bass
from concourse import mybir

ALU = mybir.AluOpType
ACT = mybir.ActivationFunctionType
AX = mybir.AxisListType
F32 = mybir.dt.float32
F32R = mybir.dt.float32r
BF16 = mybir.dt.bfloat16
I32 = mybir.dt.int32
U32 = mybir.dt.uint32

P = 128
EPS = 1e-5
SLOPE = 0.2
MASK = -1e30


def inside(n, count):
    return not isinstance(n, int) or 0 <= n < count


def through(g, par, each, of=2):
    return (g + (of - par)) * each


def hold(eng, sem):
    eng.sem_inc(sem, 1)


class Chain:

    def __init__(self, eng, sem, done):
        self.eng, self.sem, self.value = eng, sem, done

    def step(self, ins):
        ins.then_inc(self.sem, 1)
        self.value = self.value + 1

    def wait(self):
        self.eng.wait_ge(self.sem, self.value)


def wait_if(eng, sem, value):
    if not isinstance(value, int) or value > 0:
        eng.wait_ge(sem, value)


def gat_moe(nc, x, adj, W, a, gate_wT, experts, shared, out):
    T, D = x.shape
    N = adj.shape[1]
    E = gate_wT.shape[2]
    KD = D // P
    GT = 4
    TG = GT * P
    NG = T // TG
    H = 512
    KH = H // P
    WC = KD * H
    REG = T + P
    NB = 2 * T // P + E
    ST_L, ST_OH, ST_POS, ST = 0, GT * E, 3 * GT * E, 3 * GT * E + 2 * GT

    regions = nc.dram_tensor("regions", [E * REG, D], F32, kind="Internal").ap()
    x2_dram = nc.dram_tensor("x2_rows", [T, D], F32, kind="Internal").ap()
    xT_dram = nc.dram_tensor("xn2_cols", [P, NG, KD, TG], F32, kind="Internal").ap()
    y_dram = nc.dram_tensor("expert_rows", [NB * P, D], F32, kind="Internal").ap()

    with ExitStack() as top:
        def sem(name):
            return top.enter_context(nc.semaphore(name))

        def keep(name, shape, dt=F32):
            return top.enter_context(nc.sbuf_tensor(name, shape, dt))

        w_raw = keep("w_raw", [P, 2, 2 * WC])
        w_first = (sem("w_first_even"), sem("w_first_odd"))
        ident = keep("ident", [P, P])
        stash_all = keep("stash_all", [P, NG, ST])
        tile_row = keep("tile_row", [P, NB], I32)
        tile_exp = keep("tile_exp", [P, NB], I32)
        offset = keep("offset", [P, E])
        gap = keep("gap", [P, NG, GT])
        tile_num = keep("tile_num", [P, NB], I32)
        row_of = keep("row_of", [P, NG, 2 * GT], U32)
        weight_of = keep("weight_of", [P, NG, 2 * GT])
        gap_exp = keep("gap_exp", [P, NG, GT])
        xT = keep("xT", [P, 2, KD, TG])
        s_loaded = sem("s_loaded")
        xT_loaded = (sem("xT_loaded_even"), sem("xT_loaded_odd"))
        y_stored = (sem("y_stored_even"), sem("y_stored_odd"))

        part_a(nc, top, sem, locals())
        part_b(nc, top, sem, locals())
        part_c(nc, top, sem, locals())


def part_a(nc, top, sem, v):
    x, adj, W, a, gate_wT = v["x"], v["adj"], v["W"], v["a"], v["gate_wT"]
    T, D, N, E, KD, GT, TG, NG = (v[k] for k in ("T", "D", "N", "E", "KD", "GT", "TG", "NG"))
    REG, NB, WC = v["REG"], v["NB"], v["WC"]
    ST_L, ST_OH, ST_POS, ST = v["ST_L"], v["ST_OH"], v["ST_POS"], v["ST"]
    ident, stash_all, tile_row, tile_exp = v["ident"], v["stash_all"], v["tile_row"], v["tile_exp"]
    tile_num, row_of, weight_of = v["tile_num"], v["row_of"], v["weight_of"]
    w_raw, w_first, experts, offset = v["w_raw"], v["w_first"], v["experts"], v["offset"]
    regions, x2_dram, xT_dram = v["regions"], v["x2_dram"], v["xT_dram"]
    WX = D + 2

    with ExitStack() as ctx:
        def sb(name, shape, dt=F32):
            return ctx.enter_context(nc.sbuf_tensor(name, shape, dt))

        def psum(name, shape):
            return ctx.enter_context(nc.psum_tensor(name, shape, F32))

        same_graph = sb("same_graph", [P, P])
        node_of = sb("node_of", [P, N])
        before_f = sb("before_f", [P, P])
        before = sb("before", [P, P], BF16)
        ones_b = sb("ones_b", [P, P], BF16)
        lower_e = sb("lower_e", [P, E, E])
        exp_base_i = sb("exp_base_i", [P, E], I32)
        exp_base = sb("exp_base", [P, E])
        half = sb("half", [P, GT])
        jrow_i = sb("jrow_i", [P, NB], I32)
        jrow = sb("jrow", [P, NB])
        jrow128 = sb("jrow128", [P, NB])
        zero_rows = sb("zero_rows", [P, D])
        w_ext = sb("w_ext", [P, KD, WX])
        a_rows = sb("a_rows", [P, 2, D])
        wa_tmp = sb("wa_tmp", [P, D])
        gw = sb("gw", [P, KD, E])
        x_sb = sb("x_sb", [P, 2, GT, D])
        x_again = sb("x_again", [P, 2, GT, D])
        adj_sb = sb("adj_sb", [P, 2, GT, N], I32)
        stats1 = sb("stats1", [P, GT, 6])
        stats2 = sb("stats2", [P, GT, 6])
        mv1 = sb("mv1", [P, 2, GT, 2])
        mv2 = sb("mv2", [P, 2, GT, 2])
        var_eps1 = sb("var_eps1", [P, GT])
        var_eps2 = sb("var_eps2", [P, GT])
        rstd1 = sb("rstd1", [P, 2, GT])
        rstd2 = sb("rstd2", [P, 2, GT])
        shift1 = sb("shift1", [P, 2, GT])
        shift2 = sb("shift2", [P, 2, GT])
        prod1 = sb("prod1", [P, GT])
        prod2 = sb("prod2", [P, GT])
        xn = sb("xn", [P, GT, D])
        xnT = sb("xnT", [P, 2, KD, TG])
        wh = sb("wh", [P, 2, GT, WX])
        ej_diag = sb("ej_diag", [P, GT, N])
        score = sb("score", [P, GT, N])
        leaky = sb("leaky", [P, GT, N])
        mask = sb("mask", [P, GT, N])
        masked = sb("masked", [P, GT, N])
        centred = sb("centred", [P, GT, N])
        row_max = sb("row_max", [P, GT])
        row_sum = sb("row_sum", [P, GT])
        row_inv = sb("row_inv", [P, GT])
        probs = sb("probs", [P, GT, N])
        block_probs = sb("block_probs", [P, GT, P])
        probsT = sb("probsT", [P, GT, P])
        exp_z = sb("exp_z", [P, 2, 2 * D])
        relu_x = sb("relu_x", [P, 2, 2 * D])
        x2 = sb("x2", [P, 2, GT, D])
        xn2 = sb("xn2", [P, 4, GT, D])
        xn2T = sb("xn2T", [P, 2, KD, TG])
        gt = sb("gt", [P, GT, E, E])
        ge = sb("ge", [P, GT, E, E])
        rank = sb("rank", [P, GT, E])
        chosen = sb("chosen", [P, GT * E], BF16)
        stash = sb("stash", [P, ST])
        pos_e = sb("pos_e", [P, GT * E])
        pos_tmp = sb("pos_tmp", [P, 2, GT * E])
        free_row = sb("free_row", [P, E])
        scatter_row = sb("scatter_row", [P, 2, 2 * GT], U32)
        count = sb("count", [P, E])
        count_i = sb("count_i", [P, E], I32)
        tiles_i = sb("tiles_i", [P, E], I32)
        tiles = sb("tiles", [P, E])
        sums = sb("sums", [P, 4, E])
        first_tile = sb("first_tile", [P, E])
        offset_step = sb("offset_step", [P, E])
        pad_row = sb("pad_row", [P, E], I32)
        big = [sb(f"big{i}", [P, NB * E]) for i in range(2)]
        tab = sb("tab", [P, 4, NB])

        ps_T = psum("ps_T", [P, KD, TG])
        ps_W = psum("ps_W", [P, 2, 512])
        ps_E = psum("ps_E", [P, 512])
        ps_P = psum("ps_P", [P, GT, P])
        ps_Z = psum("ps_Z", [P, 2, 2 * D])
        E_SC = ps_P[:].rearrange("p t i -> p (t i)")[:, 0:GT * N]
        E_L, E_R, E_TOT = (ps_E[:, n * GT * E:(n + 1) * GT * E] for n in range(3))
        E_TOT = E_TOT[:, 0:E]

        names = ("a_const a_const2 a_wload a_wext mv1_ready ln1_ready xn_ready xnT_ready xnT_copied wh_ready "
                 "wh_copied diag_ready score_ready score_read centred_ready exp_ready probs_ready probsT_ready "
                 "probsT_copied z_ready expz_ready relu_ready x2_ready mv2_ready ln2_ready "
                 "xn2_ready xn2T_ready xn2T_copied logits_ready chosen_ready prefix_ready "
                 "rows_ready pad_ready padded "
                 "c_stats1 c_softmax c_probs c_elu c_rank c_pos c_mid c_ln1 c_ln2 c_setup c_psetup dve_held pool_held")
        S = {n: sem(n) for n in names.split()}
        for n in "a_xin a_again a_adjin x2_stored xT_stored scattered".split():
            S[n] = [sem(n + "_even"), sem(n + "_odd")]
        x_g = x.rearrange("(g t p) d -> p g t d", p=P, t=GT)
        adj_g = adj.rearrange("(g t p) j -> p g t j", p=P, t=GT)
        x2_g = x2_dram.rearrange("(g t p) d -> p g t d", p=P, t=GT)

        def one(ap, g):
            return ap[:, g] if isinstance(g, int) else ap[:, bass.ds(g, 1)].rearrange("p o t d -> p (o t) d")

        block = ctx.enter_context(nc.Block())

        def rounds(eng, body):
            for i in range(-3, 4):
                body(i, i % 4)
            with eng.Fori(0, (NG - 8) // 4) as n:
                for u in range(4):
                    body(n * 4 + (4 + u), u)
            for i in range(NG - 4, NG + 2):
                body(i, i % 4)

        @block.sync
        def _(sp):
            sp.dma_start(w_ext[:, :, 0:D], W.rearrange("(k p) f -> p k f", p=P)).then_inc(S["a_wload"], 16)
            sp.dma_start(a_rows[:], a.rearrange("(o s f) u -> o s (f u)", o=1, s=2).to_broadcast([P, 2, D])).then_inc(S["a_wload"], 16)
            for g in range(2):
                sp.dma_start(x_sb[:, g], one(x_g, g)).then_inc(S["a_xin"][g], 32)
            sp.dma_start(gw[:], gate_wT).then_inc(S["a_wload"], 16)
            for g in range(2):
                sp.dma_start(adj_sb[:, g], one(adj_g, g)).then_inc(S["a_adjin"][g], 32)
                sp.dma_start(x_again[:, g], one(x_g, g)).then_inc(S["a_again"][g], 32)

            def body(i, slot):
                par = slot % 2
                if inside(i + 4, NG) and inside(i + 2, NG):
                    sp.wait_ge(S["xn_ready"], i + 3)
                    sp.dma_start(x_sb[:, par], one(x_g, i + 4)).then_inc(S["a_xin"][par], 32)
                if inside(i + 3, NG) and inside(i + 1, NG):
                    sp.wait_ge(S["centred_ready"], i + 2)
                    sp.dma_start(adj_sb[:, 1 - par], one(adj_g, i + 3)).then_inc(S["a_adjin"][1 - par], 32)
                if inside(i - 1, NG):
                    sp.wait_ge(S["xn2T_copied"], i)
                    sp.dma_start(one(xT_dram, i - 1), xn2T[:, 1 - par]).then_inc(S["xT_stored"][1 - par], 32)
                if inside(i, NG):
                    sp.wait_ge(S["mv2_ready"], i + 1)
                    sp.dma_start(one(x2_g, i), x2[:, par]).then_inc(S["x2_stored"][par], 32)
                if inside(i + 2, NG) and inside(i, NG):
                    sp.dma_start(x_again[:, par], one(x_g, i + 2)).then_inc(S["a_again"][par], 32)

            rounds(sp, body)
            for e in range(2):
                sp.dma_start(w_raw[:, e], experts[:, e]).then_inc(w_first[e], 16)
            sp.wait_ge(S["pad_ready"], 1)
            for e in range(E):
                first = sp.value_load(pad_row[0:1, e:e + 1], min_val=0, max_val=E * REG - P)
                sp.dma_start(regions[bass.ds(first, P), :], zero_rows[:]).then_inc(S["padded"], 16)
            sp.wait_ge(S["padded"], 16 * E)
            for par in range(2):
                sp.wait_ge(S["x2_stored"][par], through(NG - 2 + par, par, 16))
                sp.wait_ge(S["xT_stored"][par], through(NG - 2 + par, par, 16))

        @block.gpsimd
        def _(pool):
            ch = Chain(pool, S["c_psetup"], 0)
            ch.step(pool.memset(ident[:], 0.0))
            ch.step(pool.memset(node_of[:], 0.0))
            ch.step(pool.memset(before_f[:], 1.0))
            ch.step(pool.memset(lower_e[:], 1.0))
            ch.step(pool.memset(half[:], -0.5))
            ch.step(pool.memset(zero_rows[:], 0.0))
            ch.step(pool.memset(block_probs[:], 0.0))
            ch.step(pool.memset(ones_b[:], 1.0))
            ch.step(pool.iota(exp_base_i[:], pattern=[[REG, E]], base=0, channel_multiplier=0))
            ch.step(pool.iota(jrow_i[:], pattern=[[1, NB]], base=0, channel_multiplier=0))
            ch.wait()
            ch.step(pool.affine_select(out=ident[:], in_=ident[:], compare_op=ALU.not_equal, fill=1.0, base=0,
                                       pattern=[[-1, P]], channel_multiplier=1))
            ch.step(pool.affine_select(out=node_of[:], in_=node_of[:], compare_op=ALU.not_equal, fill=1.0, base=0,
                                       pattern=[[-1, N]], channel_multiplier=1))
            ch.step(pool.affine_select(out=before_f[:], in_=before_f[:], compare_op=ALU.is_gt, fill=0.0, base=0,
                                       pattern=[[1, P]], channel_multiplier=-1))
            ch.step(pool.affine_select(out=lower_e[:], in_=lower_e[:], compare_op=ALU.is_gt, fill=0.0, base=0,
                                       pattern=[[1, E], [-1, E]], channel_multiplier=0))
            ch.wait()
            ch.step(pool.affine_select(out=node_of[:], in_=node_of[:], compare_op=ALU.not_equal, fill=1.0, base=-N,
                                       pattern=[[-1, N]], channel_multiplier=1))
            ch.wait()
            pool.tensor_copy(before[:], before_f[:]).then_inc(S["a_const"], 1)

            def layer_norm(g, par, mv, var_eps, rstd, prod, shift, c, ready, used, mv_ready):
                ch = Chain(pool, S[c], g * 3)
                pool.wait_ge(S[mv_ready], g + 1)
                wait_if(pool, S[used], g - 1)
                hold(pool, S["pool_held"])
                ch.step(pool.tensor_scalar(var_eps[:], mv[:, par, :, 1], EPS, None, ALU.add))
                ch.wait()
                ch.step(pool.tensor_tensor(rstd[:, par], var_eps[:], half[:], ALU.pow))
                ch.wait()
                ch.step(pool.tensor_tensor(prod[:], mv[:, par, :, 0], rstd[:, par], ALU.mult))
                ch.wait()
                hold(pool, S["pool_held"])
                pool.tensor_scalar(shift[:, par], prod[:], -1.0, None, ALU.mult).then_inc(S[ready], 1)

            def scatter(slot, par, s):
                for t in range(GT):
                    c = s * GT + t
                    pool.indirect_dma_start(
                        out=regions, out_offset=bass.IndirectOffsetOnAxis(ap=scatter_row[:, par, c:c + 1], axis=0),
                        in_=xn2[:, slot, t, :], in_offset=None).then_inc(S["scattered"][par], 32)

            def body(i, slot):
                par = slot % 2
                last_norm = isinstance(i, int) and i == NG - 1
                if inside(i + 3, NG):
                    layer_norm(i + 3, 1 - par, mv1, var_eps1, rstd1, prod1, shift1, "c_ln1", "ln1_ready", "xn_ready", "mv1_ready")
                if inside(i - 2, NG):
                    pool.wait_ge(S["rows_ready"], i - 1)
                    hold(pool, S["pool_held"])
                    scatter((slot + 2) % 4, par, 0)
                    if not last_norm:
                        scatter((slot + 2) % 4, par, 1)
                if inside(i, NG):
                    layer_norm(i, par, mv2, var_eps2, rstd2, prod2, shift2, "c_ln2", "ln2_ready", "xn2_ready", "mv2_ready")
                if last_norm:
                    scatter((slot + 2) % 4, par, 1)

            rounds(pool, body)
            for par in range(2):
                pool.wait_ge(S["scattered"][par], through(NG - 2 + par, par, 16 * 2 * GT))

        @block.scalar
        def _(act):
            def normed(g, par, dst, src, rstd, shift, ln_ready, ready):
                act.wait_ge(S[ln_ready], g + 1)
                for t in range(GT):
                    last = act.activation(dst[:, t], src[:, par, t], ACT.Identity,
                                          bias=shift[:, par, t:t + 1], scale=rstd[:, par, t:t + 1])
                last.then_inc(S[ready], 1)

            def keep_wh(g, par, t):
                act.wait_ge(S["wh_ready"], g * GT + (t + 1))
                act.copy(wh[:, par, t], ps_W[:, t % 2, 0:WX]).then_inc(S["wh_copied"], 1)

            def body(i, slot):
                par = slot % 2
                U, X, Y, V, Q = i + 3, i + 2, i + 1, i, i - 1
                hasU, hasX, hasY, hasV, hasQ = (inside(g, NG) for g in (U, X, Y, V, Q))
                if hasV:
                    for h in range(2):
                        act.wait_ge(S["z_ready"], V * 2 + (h + 1))
                        wait_if(act, S["x2_ready"], (V - 1) * 2 + (h + 1))
                        act.activation(exp_z[:, h], ps_Z[:, h], ACT.Exp).then_inc(S["expz_ready"], 1)
                if hasQ:
                    wait_if(act, S["xn2T_ready"], Q - 3)
                    wait_if(act, S["scattered"][1 - par], through(Q - 4, 1 - par, 16 * 2 * GT))
                    normed(Q, 1 - par, xn2[:, (slot + 3) % 4], x2, rstd2, shift2, "ln2_ready", "xn2_ready")
                if hasX:
                    wait_if(act, S["z_ready"], (X - 1) * 2)
                    keep_wh(X, par, 0)
                    keep_wh(X, par, 1)
                if hasQ:
                    act.wait_ge(S["xn2T_ready"], Q + 1)
                    wait_if(act, S["logits_ready"], Q - 1)
                    wait_if(act, S["xT_stored"][1 - par], through(Q - 2, 1 - par, 16))
                    for k in range(KD):
                        last = act.copy(xn2T[:, 1 - par, k], ps_T[:, k])
                    last.then_inc(S["xn2T_copied"], 1)
                if hasX:
                    keep_wh(X, par, 2)
                if hasU:
                    wait_if(act, S["xnT_ready"], U)
                    normed(U, 1 - par, xn, x_sb, rstd1, shift1, "ln1_ready", "xn_ready")
                if hasY:
                    act.wait_ge(S["centred_ready"], Y + 1)
                    act.activation(probs[:], centred[:], ACT.Exp).then_inc(S["exp_ready"], 1)
                if hasX:
                    keep_wh(X, par, 3)
                if hasU:
                    act.wait_ge(S["xnT_ready"], U + 1)
                    wait_if(act, S["wh_ready"], (U - 1) * GT)
                    for k in range(KD):
                        last = act.copy(xnT[:, 1 - par, k], ps_T[:, k])
                    last.then_inc(S["xnT_copied"], 1)
                if hasY:
                    act.wait_ge(S["probsT_ready"], Y + 1)
                    wait_if(act, S["z_ready"], Y * 2)
                    act.copy(probsT[:], ps_P[:]).then_inc(S["probsT_copied"], 1)

            rounds(act, body)

        @block.tensor
        def _(pe):
            pe.wait_ge(S["a_const"], 1)
            pe.wait_ge(S["a_wext"], 1)

            def prefixes(g):
                pe.wait_ge(S["chosen_ready"], g + 1)
                pe.matmul(E_R, before[:], chosen[:], start=True, stop=False)
                for t in range(1, GT):
                    pe.matmul(E_R[:, t * E:], ones_b[:], chosen[:, 0:(GT - t) * E], start=False, stop=(t == GT - 1))
                for t in range(GT):
                    last = pe.matmul(E_TOT, ones_b[:], chosen[:, t * E:(t + 1) * E], start=(t == 0), stop=(t == GT - 1))
                last.then_inc(S["prefix_ready"], 1)

            def wh_tile(g, par, t):
                wait_if(pe, S["wh_copied"], g * GT + (t - 1))
                for k in range(KD):
                    last = pe.matmul(ps_W[:, t % 2, 0:WX], xnT[:, par, k, t * P:(t + 1) * P], w_ext[:, k],
                                     start=(k == 0), stop=(k == KD - 1))
                last.then_inc(S["wh_ready"], 1)

            def body(i, slot):
                par = slot % 2
                U, X, Y, V, Q, Z = i + 3, i + 2, i + 1, i, i - 1, i - 2
                hasU, hasX, hasY, hasV, hasQ, hasZ = (inside(g, NG) for g in (U, X, Y, V, Q, Z))
                if hasV:
                    pe.wait_ge(S["probsT_copied"], V + 1)
                    for t in range(GT):
                        if t % 2 == 0:
                            wait_if(pe, S["relu_ready"], (V - 1) * 2 + (t // 2 + 1))
                        last = pe.matmul(ps_Z[:, t // 2, (t % 2) * D:(t % 2 + 1) * D], probsT[:, t], wh[:, par, t, 0:D],
                                         start=True, stop=True)
                        if t % 2 == 1:
                            last.then_inc(S["z_ready"], 1)
                if hasY:
                    pe.wait_ge(S["diag_ready"], Y + 1)
                    wait_if(pe, S["probsT_copied"], Y)
                    pe.matmul(E_SC, same_graph[:], ej_diag[:].rearrange("p t j -> p (t j)"),
                              start=True, stop=True).then_inc(S["score_ready"], 1)
                if hasX:
                    pe.wait_ge(S["xnT_copied"], X + 1)
                    wh_tile(X, par, 0)
                    wh_tile(X, par, 1)
                if hasZ:
                    prefixes(Z)
                if hasQ:
                    pe.wait_ge(S["xn2_ready"], Q + 1)
                    pe.wait_ge(S["xnT_copied"], min(Q + 4, NG) if isinstance(Q, int) else Q + 4)
                    for k in range(KD):
                        for t in range(GT):
                            last = pe.transpose(ps_T[:, k, t * P:(t + 1) * P], xn2[:, (slot + 3) % 4, t, k * P:(k + 1) * P], ident[:])
                    last.then_inc(S["xn2T_ready"], 1)
                if hasX:
                    wh_tile(X, par, 2)
                if hasQ:
                    pe.wait_ge(S["xn2T_copied"], Q + 1)
                    wait_if(pe, S["rows_ready"], Q)
                    for t in range(GT):
                        for k in range(KD):
                            last = pe.matmul(E_L[:, t * E:(t + 1) * E], xn2T[:, 1 - par, k, t * P:(t + 1) * P], gw[:, k],
                                             start=(k == 0), stop=(k == KD - 1))
                    last.then_inc(S["logits_ready"], 1)
                if hasU:
                    pe.wait_ge(S["xn_ready"], U + 1)
                    for k in range(KD):
                        for t in range(GT):
                            last = pe.transpose(ps_T[:, k, t * P:(t + 1) * P], xn[:, t, k * P:(k + 1) * P], ident[:])
                    last.then_inc(S["xnT_ready"], 1)
                if hasX:
                    wh_tile(X, par, 3)
                if hasY:
                    pe.wait_ge(S["probs_ready"], Y + 1)
                    for t in range(GT):
                        last = pe.transpose(ps_P[:, t], block_probs[:, t], ident[:])
                    last.then_inc(S["probsT_ready"], 1)

            rounds(pe, body)

        @block.vector
        def _(dve):
            ch = Chain(dve, S["c_setup"], 0)
            ch.step(dve.memset(same_graph[:], 0.0))
            ch.wait()
            ch.step(dve.memset(same_graph[0:N, 0:N], 1.0))
            ch.step(dve.memset(same_graph[N:P, N:P], 1.0))
            dve.wait_ge(S["a_wload"], 48)
            for k in range(KD):
                for s in range(2):
                    ch.step(dve.tensor_tensor_reduce(wa_tmp[:], w_ext[:, k, 0:D], a_rows[:, s], 1.0, 0.0, ALU.mult, ALU.add,
                                                     w_ext[:, k, D + s:D + s + 1]))
                    ch.wait()
            dve.wait_ge(S["a_const"], 1)
            ch.step(dve.tensor_copy(exp_base[:], exp_base_i[:]))
            ch.step(dve.tensor_copy(free_row[:], exp_base_i[:]))
            ch.step(dve.tensor_copy(jrow[:], jrow_i[:]))
            ch.wait()
            ch.step(dve.tensor_scalar(jrow128[:], jrow[:], float(P), None, ALU.mult))
            ch.wait()
            dve.memset(wa_tmp[:, 0:1], 0.0).then_inc(S["a_wext"], 1)

            def spread(ap, n):
                return ap.unsqueeze(2).to_broadcast([P, GT, n])

            def diag(g, par):
                dve.wait_ge(S["wh_copied"], (g + 1) * GT)
                dve.tensor_tensor(ej_diag[:], node_of[:].unsqueeze(1).to_broadcast([P, GT, N]),
                                  wh[:, par, :, D + 1:D + 2].to_broadcast([P, GT, N]), ALU.mult).then_inc(S["diag_ready"], 1)

            def softmax_out(g):
                ch = Chain(dve, S["c_probs"], g * 2)
                dve.wait_ge(S["exp_ready"], g + 1)
                ch.step(dve.tensor_reduce(row_sum[:], probs[:], AX.X, ALU.add))
                ch.wait()
                ch.step(dve.reciprocal(row_inv[:], row_sum[:]))
                ch.wait()
                wait_if(dve, S["probsT_ready"], g)
                for h in range(2):
                    r = slice(h * N, (h + 1) * N)
                    last = dve.tensor_tensor(block_probs[r, :, h * N:(h + 1) * N], probs[r],
                                             row_inv[r].unsqueeze(2).to_broadcast([N, GT, N]), ALU.mult)
                last.then_inc(S["probs_ready"], 1)

            def stats_and_choice(U, Z, par_u, hasU, hasZ):
                if hasU:
                    cs = Chain(dve, S["c_stats1"], U * GT)
                    wait_if(dve, S["mv1_ready"], U)
                    dve.wait_ge(S["a_xin"][par_u], through(U, par_u, 16))

                def stat(t):
                    if hasU:
                        cs.step(dve.bn_stats(stats1[:, t], x_sb[:, par_u, t]))

                if hasZ:
                    ch = Chain(dve, S["c_rank"], Z * 8)
                    wait_if(dve, S["c_pos"], Z * 5)
                    dve.wait_ge(S["logits_ready"], Z + 1)
                    L = stash[:, ST_L:ST_L + GT * E].rearrange("p (t e) -> p t e", t=GT)
                    ch.step(dve.tensor_copy(stash[:, ST_L:ST_L + GT * E], E_L))
                    other = L.unsqueeze(2).to_broadcast([P, GT, E, E])
                    own = L.unsqueeze(3).to_broadcast([P, GT, E, E])
                stat(0)
                if hasZ:
                    ch.wait()
                    ch.step(dve.tensor_tensor(ge[:], other, own, ALU.is_ge))
                    ch.step(dve.tensor_tensor(gt[:], other, own, ALU.is_gt))
                    dve.wait_ge(S["c_rank"], Z * 8 + 2)
                    ch.step(dve.tensor_tensor(ge[:], ge[:], lower_e[:].unsqueeze(1).to_broadcast([P, GT, E, E]), ALU.mult))
                stat(1)
                if hasZ:
                    ch.wait()
                    ch.step(dve.tensor_tensor(gt[:], gt[:], ge[:], ALU.max))
                stat(2)
                if hasZ:
                    ch.wait()
                    ch.step(dve.tensor_reduce(rank[:], gt[:], AX.X, ALU.add))
                stat(3)
                if hasZ:
                    ch.wait()
                    R = rank[:].rearrange("p t e -> p (t e)")
                    dve.tensor_scalar(chosen[:], R, 2.0, None, ALU.is_lt).then_inc(S["chosen_ready"], 1)
                    for s in range(2):
                        ch.step(dve.tensor_scalar(stash[:, ST_OH + s * GT * E:ST_OH + (s + 1) * GT * E], R, float(s), None, ALU.is_equal))
                if hasU:
                    cs.wait()
                    wait_if(dve, S["ln1_ready"], U - 1)
                    hold(dve, S["dve_held"])
                    for t in range(GT):
                        last = dve.bn_aggr(mv1[:, par_u, t], stats1[:, t])
                    last.then_inc(S["mv1_ready"], 1)

            def place(g, par):
                ch = Chain(dve, S["c_pos"], g * 5)
                dve.wait_ge(S["c_rank"], (g + 1) * 8)
                dve.wait_ge(S["prefix_ready"], g + 1)
                ch.step(dve.tensor_tensor(pos_e[:].rearrange("p (t e) -> p t e", t=GT), E_R.rearrange("p (t e) -> p t e", t=GT),
                                          free_row[:].unsqueeze(1).to_broadcast([P, GT, E]), ALU.add))
                ch.wait()
                ch.step(dve.tensor_tensor(free_row[:], free_row[:], E_TOT, ALU.add))
                ch.step(dve.tensor_tensor(pos_tmp[:], stash[:, ST_OH:ST_POS].rearrange("p (s c) -> p s c", s=2),
                                          pos_e[:].unsqueeze(1).to_broadcast([P, 2, GT * E]), ALU.mult))
                ch.wait()
                ch.step(dve.tensor_reduce(stash[:, ST_POS:ST], pos_tmp[:].rearrange("p s (t e) -> p (s t) e", e=E), AX.X, ALU.add))
                ch.wait()
                wait_if(dve, S["scattered"][par], through(g - 2, par, 16 * 2 * GT))
                dve.tensor_copy(scatter_row[:, par], stash[:, ST_POS:ST]).then_inc(S["rows_ready"], 1)
                if isinstance(g, int):
                    dst = stash_all[:, g]
                else:
                    dst = stash_all[:, bass.ds(g, 1)].rearrange("p o c -> p (o c)")
                ch.step(dve.tensor_copy(dst, stash[:]))

            def softmax_place_elu(Y, Z, V, par, hasY, hasZ, hasV):
                if hasY:
                    ch = Chain(dve, S["c_softmax"], Y * 4)
                    dve.wait_ge(S["a_adjin"][1 - par], through(Y, 1 - par, 16))
                    ch.step(dve.tensor_scalar(mask[:], adj_sb[:, 1 - par], 0.0, MASK, ALU.is_equal, ALU.mult))
                    dve.wait_ge(S["score_ready"], Y + 1)
                    dve.tensor_tensor(score[:], E_SC.rearrange("p (t j) -> p t j", t=GT),
                                      wh[:, 1 - par, :, D:D + 1].to_broadcast([P, GT, N]), ALU.add).then_inc(S["score_read"], 1)

                def relu(h):
                    if hasV:
                        ts = slice(2 * h, 2 * h + 2)
                        dve.wait_ge(S["expz_ready"], V * 2 + (h + 1))
                        dve.scalar_tensor_tensor(out=relu_x[:, h], in0=ps_Z[:, h], scalar=0.0,
                                                 in1=x_again[:, par, ts].rearrange("p t d -> p (t d)"),
                                                 op0=ALU.max, op1=ALU.add).then_inc(S["relu_ready"], 1)

                def x2_half(h):
                    if hasV:
                        ts = slice(2 * h, 2 * h + 2)
                        dve.wait_ge(S["relu_ready"], V * 2 + (h + 1))
                        dve.scalar_tensor_tensor(out=x2[:, par, ts].rearrange("p t d -> p (t d)"), in0=exp_z[:, h], scalar=1.0,
                                                 in1=relu_x[:, h], op0=ALU.min, op1=ALU.add).then_inc(S["x2_ready"], 1)

                if hasV:
                    dve.wait_ge(S["a_again"][par], through(V, par, 16))
                    wait_if(dve, S["xn2_ready"], V - 1)
                    wait_if(dve, S["x2_stored"][par], through(V - 2, par, 16))
                relu(0)
                if hasZ:
                    place(Z, par)
                if hasY:
                    dve.wait_ge(S["score_read"], Y + 1)
                    ch.step(dve.scalar_tensor_tensor(out=leaky[:], in0=score[:], scalar=SLOPE, in1=score[:], op0=ALU.mult, op1=ALU.max))
                x2_half(0)
                if hasY:
                    ch.wait()
                    ch.step(dve.tensor_tensor(masked[:], leaky[:], mask[:], ALU.add))
                relu(1)
                if hasY:
                    ch.wait()
                    ch.step(dve.tensor_reduce(row_max[:], masked[:], AX.X, ALU.max))
                x2_half(1)
                if hasY:
                    ch.wait()
                    dve.tensor_tensor(centred[:], masked[:], spread(row_max[:], N), ALU.subtract).then_inc(S["centred_ready"], 1)
                if hasV:
                    ce = Chain(dve, S["c_elu"], V * GT)
                    dve.wait_ge(S["x2_ready"], V * 2 + 2)
                    for t in range(GT):
                        ce.step(dve.bn_stats(stats2[:, t], x2[:, par, t]))
                    ce.wait()
                    wait_if(dve, S["ln2_ready"], V - 1)
                    hold(dve, S["dve_held"])
                    for t in range(GT):
                        last = dve.bn_aggr(mv2[:, par, t], stats2[:, t])
                    last.then_inc(S["mv2_ready"], 1)

            def body(i, slot):
                par = slot % 2
                U, Y, V, Z = i + 3, i + 1, i, i - 2
                hasU, hasY, hasV, hasZ = (inside(g, NG) for g in (U, Y, V, Z))
                if hasY:
                    diag(Y, 1 - par)
                if hasU or hasZ:
                    stats_and_choice(U, Z, 1 - par, hasU, hasZ)
                if hasZ or hasY or hasV:
                    softmax_place_elu(Y, Z, V, par, hasY, hasZ, hasV)
                if hasY:
                    softmax_out(Y)

            rounds(dve, body)

            ch = Chain(dve, S["c_mid"], 0)

            def do(ins):
                ch.step(ins)
                ch.wait()

            do(dve.tensor_tensor(count[:], free_row[:], exp_base[:], ALU.subtract))
            dve.tensor_copy(pad_row[:], free_row[:]).then_inc(S["pad_ready"], 1)
            do(dve.tensor_scalar(count_i[:], count[:], float(P - 1), None, ALU.add))
            do(dve.tensor_scalar(tiles_i[:], count_i[:], 7, None, ALU.logical_shift_right))
            do(dve.tensor_copy(tiles[:], tiles_i[:]))
            do(dve.tensor_copy(sums[:, 0], tiles_i[:]))
            for n, d in enumerate((1, 2, 4)):
                do(dve.tensor_copy(sums[:, n + 1, 0:d], sums[:, n, 0:d]))
                do(dve.tensor_tensor(sums[:, n + 1, d:E], sums[:, n, d:E], sums[:, n, 0:E - d], ALU.add))
            end_tile = sums[:, 3]
            do(dve.tensor_tensor(first_tile[:], end_tile, tiles[:], ALU.subtract))
            do(dve.scalar_tensor_tensor(out=offset[:], in0=first_tile[:], scalar=-float(P), in1=exp_base[:], op0=ALU.mult, op1=ALU.add))
            b = [t[:].rearrange("p (j e) -> p j e", e=E) for t in big]

            def by_e(ap):
                return ap.unsqueeze(1).to_broadcast([P, NB, E])

            def by_j(ap):
                return ap.unsqueeze(2).to_broadcast([P, NB, E])

            do(dve.tensor_copy(offset_step[:, 0:1], offset[:, 0:1]))
            do(dve.tensor_tensor(offset_step[:, 1:E], offset[:, 1:E], offset[:, 0:E - 1], ALU.subtract))
            do(dve.tensor_tensor(b[0], by_j(jrow[:]), by_e(first_tile[:]), ALU.is_ge))
            ch.step(dve.tensor_reduce(tab[:, 1], b[0], AX.X, ALU.add))
            do(dve.tensor_tensor(b[1], b[0], by_e(offset_step[:]), ALU.mult))
            do(dve.tensor_reduce(tab[:, 0], b[1], AX.X, ALU.add))
            do(dve.tensor_tensor(tab[:, 0], tab[:, 0], jrow128[:], ALU.add))
            do(dve.tensor_scalar(tab[:, 2], jrow[:], end_tile[:, E - 1:E], None, ALU.is_lt))
            do(dve.scalar_tensor_tensor(out=tab[:, 3], in0=tab[:, 0], scalar=-float((E - 1) * REG), in1=tab[:, 2], op0=ALU.add, op1=ALU.mult))
            do(dve.tensor_scalar(tile_row[:], tab[:, 3], float((E - 1) * REG), None, ALU.add))
            do(dve.tensor_scalar(tile_exp[:], tab[:, 1], -1.0, float(2 * WC), ALU.add, ALU.mult))
            do(dve.tensor_copy(tile_num[:], tab[:, 1]))


def part_b(nc, top, sem, v):
    experts, E, D, KD, H, KH, WC, NB = (v[k] for k in ("experts", "E", "D", "KD", "H", "KH", "WC", "NB"))
    ident, tile_row, tile_exp, tile_num, regions, y_dram = (v[k] for k in ("ident", "tile_row", "tile_exp", "tile_num", "regions", "y_dram"))
    REG, NG, GT, stash_all, offset = (v[k] for k in ("REG", "NG", "GT", "stash_all", "offset"))
    ST_L, ST_OH, ST_POS, ST = (v[k] for k in ("ST_L", "ST_OH", "ST_POS", "ST"))
    w_raw, w_first, row_of, gap, gap_exp = (v[k] for k in ("w_raw", "w_first", "row_of", "gap", "gap_exp"))
    xT, xT_loaded, xT_dram, shared, s_loaded, y_stored = (v[k] for k in ("xT", "xT_loaded", "xT_dram", "shared", "s_loaded", "y_stored"))
    with ExitStack() as ctx:
        def sb(name, shape, dt=F32):
            return ctx.enter_context(nc.sbuf_tensor(name, shape, dt))

        def psum(name, shape):
            return ctx.enter_context(nc.psum_tensor(name, shape, F32))

        w_hi = sb("w_hi", [P, E * 2 * WC], F32R)
        w_lo = sb("w_lo", [P, E * 2 * WC], F32R)
        rows = sb("rows", [P, 4, D])
        xT_hi = sb("xT_hi", [P, 2, KD, P], F32R)
        xT_lo = sb("xT_lo", [P, 2, KD, P], F32R)
        hid = sb("hid", [P, 2, H])
        hT_hi = sb("hT_hi", [P, 2, KH, P], F32R)
        hT_lo = sb("hT_lo", [P, 2, KH, P], F32R)
        y_sb = sb("y_sb", [P, 2, D])
        picked = sb("picked", [P, NG * 2 * GT * E])
        picked_sum = sb("picked_sum", [P, NG, 2 * GT])
        v_top = sb("v_top", [P, NG, 2, GT])
        ps_X = psum("ps_X", [P, 512])
        ps_H = psum("ps_H", [P, 2, H])
        ps_HT = psum("ps_HT", [P, 2, KH, P])
        ps_Y = psum("ps_Y", [P, 2, 512])

        names = ("w_first_hi w_first_split w_split_hi w_split xT_ready xhi_ready xlo_ready h_ready silu_ready hT_ready "
                 "hhi_ready hlo_ready y_ready y_copied tables")
        S = {n: sem("b_" + n) for n in names.split()}
        S["w_loaded"] = [sem("b_w_loaded_even"), sem("b_w_loaded_odd")]
        S["rows_loaded"] = [sem(f"b_rows_loaded_{n}") for n in range(4)]
        S["y_stored"] = y_stored
        block = ctx.enter_context(nc.Block())

        EARLY = 6
        TABLE_STEPS = 8

        def steps(eng, body, by_weights=False):
            for j in range(-1, 4):
                body(j, j % 4, *([True] * by_weights))
            if by_weights:
                with eng.Fori(0, EARLY) as n:
                    for u in range(4):
                        body(n * 4 + (4 + u), u, True)
                eng.wait_ge(S["w_split"], E)
                with eng.Fori(EARLY, (NB - 8) // 4) as n:
                    for u in range(4):
                        body(n * 4 + (4 + u), u)
            else:
                with eng.Fori(0, (NB - 8) // 4) as n:
                    for u in range(4):
                        body(n * 4 + (4 + u), u)
            for j in range(NB - 4, NB + 2):
                body(j, j % 4)

        @block.sync
        def _(sp):
            def load(j, slot):
                r = sp.value_load(tile_row[0:1, bass.ds(j, 1)], min_val=0, max_val=E * REG - P)
                sp.dma_start(rows[:, slot], regions[bass.ds(r, P), :]).then_inc(S["rows_loaded"][slot], 64)

            def body(j, slot):
                par = slot % 2
                if inside(j + 3, NB) and (not isinstance(j, int) or j >= 0):
                    wait_if(sp, S["xT_ready"], j)
                    load(j + 3, (slot + 3) % 4)
                if inside(j - 2, NB):
                    sp.wait_ge(S["y_copied"], j - 1)
                    row = (j - 2) * P
                    dst = y_dram[row:row + P] if isinstance(j, int) else y_dram[bass.ds(row, P)]
                    sp.dma_start(dst, y_sb[:, par]).then_inc(S["y_stored"][par], 32)

            for j in range(3):
                load(j, j)
            for g in range(2):
                sp.dma_start(xT[:, g], xT_dram[:, g]).then_inc(xT_loaded[g], 32)
            steps(sp, body)

        @block.gpsimd
        def _(pool):
            pool.wait_ge(w_first[1], 16)
            pool.wait_ge(S["w_first_split"], 1)
            pool.dma_start(w_raw[:, 0], experts[:, 2]).then_inc(S["w_loaded"][0], 16)
            pool.sem_inc(S["w_split"], 1)
            for e in range(1, E):
                c = slice(e * 2 * WC, (e + 1) * 2 * WC)
                if e >= 2:
                    pool.wait_ge(S["w_loaded"][e % 2], 16 * (e // 2))
                pool.tensor_copy(w_hi[:, c], w_raw[:, e % 2]).then_inc(S["w_split_hi"], 1)
                pool.wait_ge(S["w_split_hi"], e)
                pool.tensor_tensor(w_lo[:, c], w_raw[:, e % 2], w_hi[:, c].bitcast(F32), ALU.subtract).then_inc(S["w_split"], 1)
                if e + 2 < E:
                    pool.wait_ge(S["w_split"], e + 1)
                    pool.dma_start(w_raw[:, e % 2], experts[:, e + 2]).then_inc(S["w_loaded"][e % 2], 16)
            pool.wait_ge(S["w_split"], E)
            pool.dma_start(w_raw[:].rearrange("p e c -> p (e c)")[:, 0:3 * WC], shared).then_inc(s_loaded, 16)
            pool.wait_ge(s_loaded, 16)

        @block.scalar
        def _(act):
            def body(j, slot):
                par = slot % 2
                if inside(j, NB):
                    act.wait_ge(S["h_ready"], j + 1)
                    act.activation(hid[:, par], ps_H[:, par], ACT.Silu).then_inc(S["silu_ready"], 1)
                if inside(j + 1, NB):
                    act.wait_ge(S["xT_ready"], j + 2)
                    act.copy(xT_hi[:, 1 - par].rearrange("p k t -> p (k t)"), ps_X[:, 0:D]).then_inc(S["xhi_ready"], 1)
                if inside(j - 1, NB):
                    act.wait_ge(S["hT_ready"], j)
                    wait_if(act, S["y_ready"], j - 2)
                    act.copy(hT_hi[:, 1 - par], ps_HT[:, 1 - par]).then_inc(S["hhi_ready"], 1)

            act.wait_ge(w_first[0], 16)
            act.copy(w_hi[:, 0:2 * WC], w_raw[:, 0]).then_inc(S["w_first_hi"], 1)
            steps(act, body)
            act.wait_ge(S["tables"], TABLE_STEPS)
            act.activation(gap_exp[:], gap[:], ACT.Exp)

        @block.vector
        def _(dve):
            def tables(n):
                oh = stash_all[:, :, ST_OH:ST_POS].rearrange("p g (c e) -> p g c e", e=E)
                by_c = picked[:].rearrange("p (g c e) -> p g c e", e=E, g=NG)
                half = picked[:, 0:NG * GT * E]
                if n > 0:
                    dve.wait_ge(S["tables"], n)
                if n == 0:
                    ins = dve.tensor_tensor(by_c, oh, offset[:].unsqueeze(1).unsqueeze(1).to_broadcast([P, NG, 2 * GT, E]), ALU.mult)
                elif n == 1:
                    ins = dve.tensor_reduce(picked_sum[:], by_c, AX.X, ALU.add)
                elif n == 2:
                    ins = dve.tensor_tensor(row_of[:], stash_all[:, :, ST_POS:ST], picked_sum[:], ALU.subtract)
                elif n in (3, 5):
                    s = (n - 3) // 2
                    ins = dve.tensor_tensor(half.rearrange("p (g c) -> p g c", g=NG),
                                            stash_all[:, :, ST_OH + s * GT * E:ST_OH + (s + 1) * GT * E],
                                            stash_all[:, :, ST_L:ST_L + GT * E], ALU.mult)
                elif n in (4, 6):
                    ins = dve.tensor_reduce(v_top[:, :, (n - 4) // 2], half.rearrange("p (g t e) -> p g t e", g=NG, e=E), AX.X, ALU.add)
                else:
                    ins = dve.tensor_tensor(gap[:], v_top[:, :, 1], v_top[:, :, 0], ALU.subtract)
                ins.then_inc(S["tables"], 1)

            def body(j, slot):
                par = slot % 2
                if inside(j + 1, NB):
                    dve.wait_ge(S["xhi_ready"], j + 2)
                    q = xT_hi[:, 1 - par].rearrange("p k t -> p (k t)")
                    dve.tensor_tensor(xT_lo[:, 1 - par].rearrange("p k t -> p (k t)"), ps_X[:, 0:D], q.bitcast(F32),
                                      ALU.subtract).then_inc(S["xlo_ready"], 1)
                if inside(j - 1, NB):
                    dve.wait_ge(S["hhi_ready"], j)
                    dve.tensor_tensor(hT_lo[:, 1 - par], ps_HT[:, 1 - par], hT_hi[:, 1 - par].bitcast(F32),
                                      ALU.subtract).then_inc(S["hlo_ready"], 1)
                if inside(j - 2, NB):
                    dve.wait_ge(S["y_ready"], j - 1)
                    wait_if(dve, S["y_stored"][par], through(j - 4, par, 16))
                    dve.tensor_copy(y_sb[:, par], ps_Y[:, par, 0:D]).then_inc(S["y_copied"], 1)
                if isinstance(j, int) and NB - 4 <= j < NB:
                    for n in range(2):
                        tables((j - NB + 4) * 2 + n)

            dve.wait_ge(S["w_first_hi"], 1)
            dve.tensor_tensor(w_lo[:, 0:2 * WC], w_raw[:, 0], w_hi[:, 0:2 * WC].bitcast(F32), ALU.subtract).then_inc(S["w_first_split"], 1)
            steps(dve, body)
        @block.tensor
        def _(pe):
            start_of = [pe.alloc_register(f"weights_{n}") for n in range(4)]

            def start(slot):
                return pe.snap(start_of[slot % 4], min_val=0, max_val=(E - 1) * 2 * WC)

            def body(j, slot, waiting=False):
                par = slot % 2
                if inside(j, NB):
                    base = start(slot)
                if inside(j - 2, NB):
                    base2 = start(slot - 2)
                if inside(j, NB) and waiting:
                    pe.wait_ge(S["w_split"], pe.value_load(tile_num[0:1, bass.ds(j, 1)], min_val=1, max_val=E))
                if inside(j, NB):
                    pe.wait_ge(S["xlo_ready"], j + 1)
                    n = 0
                    for k in range(KD):
                        for lhs, rhs in ((xT_hi, w_hi), (xT_lo, w_hi), (xT_hi, w_lo)):
                            last = pe.matmul(ps_H[:, par], lhs[:, par, k], rhs[:, bass.ds(base + k * H, H)],
                                             start=(n == 0), stop=(n == 3 * KD - 1))
                            n += 1
                    last.then_inc(S["h_ready"], 1)
                if inside(j - 1, NB):
                    pe.wait_ge(S["silu_ready"], j)
                    for k in range(KH):
                        last = pe.transpose(ps_HT[:, 1 - par, k], hid[:, 1 - par, k * P:(k + 1) * P], ident[:])
                    last.then_inc(S["hT_ready"], 1)
                if inside(j + 1, NB):
                    nxt = (slot + 1) % 4
                    pe.wait_ge(S["rows_loaded"][nxt], through(j + 1, nxt, 16, of=4))
                    for k in range(KD):
                        last = pe.transpose(ps_X[:, k * P:(k + 1) * P], rows[:, nxt, k * P:(k + 1) * P], ident[:])
                    last.then_inc(S["xT_ready"], 1)
                if inside(j - 2, NB):
                    pe.wait_ge(S["hlo_ready"], j - 1)
                    wait_if(pe, S["y_copied"], j - 3)
                    n = 0
                    for k in range(KH):
                        for lhs, rhs in ((hT_hi, w_hi), (hT_lo, w_hi), (hT_hi, w_lo)):
                            last = pe.matmul(ps_Y[:, par, 0:D], lhs[:, par, k], rhs[:, bass.ds(base2 + (WC + k * D), D)],
                                             start=(n == 0), stop=(n == 3 * KH - 1))
                            n += 1
                    last.then_inc(S["y_ready"], 1)
                if inside(j + 1, NB):
                    pe.reg_load(start_of[(slot + 1) % 4], tile_exp[0:1, bass.ds(j + 1, 1)])

            steps(pe, body, True)


def part_c(nc, top, sem, v):
    shared, D, KD, H, KH, WC, NG, GT, TG = (v[k] for k in ("shared", "D", "KD", "H", "KH", "WC", "NG", "GT", "TG"))
    row_of, weight_of, y_dram, x2_dram, xT_dram, out = (v[k] for k in ("row_of", "weight_of", "y_dram", "x2_dram", "xT_dram", "out"))
    w_raw, gap_exp, xT, xT_loaded, y_stored, NB = (v[k] for k in ("w_raw", "gap_exp", "xT", "xT_loaded", "y_stored", "NB"))
    with ExitStack() as ctx:
        def sb(name, shape, dt=F32):
            return ctx.enter_context(nc.sbuf_tensor(name, shape, dt))

        def psum(name, shape):
            return ctx.enter_context(nc.psum_tensor(name, shape, F32))

        gap_sum = sb("gap_sum", [P, NG, GT])
        gap_inv = sb("gap_inv", [P, NG, GT])
        s_raw = w_raw[:].rearrange("p e (m c) -> p (e m) c", c=WC)
        s_hi = sb("s_hi", [P, 3, WC], F32R)
        s_lo = sb("s_lo", [P, 3, WC], F32R)
        xT_h = sb("xT_h", [P, 2, KD, TG], F32R)
        xT_l = sb("xT_l", [P, 2, KD, TG], F32R)
        x2_in = sb("x2_in", [P, 2, GT, D])
        gate = sb("gate", [P, 2, TG])
        hidT = sb("hidT", [P, 2, TG])
        hidT_h = sb("hidT_h", [P, 2, KH, TG], F32R)
        hidT_l = sb("hidT_l", [P, 2, KH, TG], F32R)
        rows_l = sb("rows_l", [P, 2, 2 * GT], U32)
        weights_l = sb("weights_l", [P, 2, 2 * GT])
        y_in = sb("y_in", [P, 2, 2, GT, D])
        out_sb = sb("out_sb", [P, 2, GT, D])
        ps_G = psum("ps_G", [P, 2, TG])
        ps_U = psum("ps_U", [P, 2, TG])
        ps_D = psum("ps_D", [P, 2, 2, D])

        names = ("s_hi_ready s_split xhi_ready xlo_ready gate_ready up_ready silu_ready "
                 "hid_ready hhi_ready hlo_ready down_ready idx_ready first_ready out_ready c_comb held weights")
        S = {n: sem("c_" + n) for n in names.split()}
        for n in "x2_loaded gathered stored".split():
            S[n] = [sem(f"c_{n}_even"), sem(f"c_{n}_odd")]
        S["xT_loaded"] = xT_loaded
        x2_g = x2_dram.rearrange("(g t p) d -> p g t d", p=P, t=GT)
        out_g = out.rearrange("(g t p) d -> p g t d", p=P, t=GT)

        def one(ap, g):
            return ap[:, g] if isinstance(g, int) else ap[:, bass.ds(g, 1)].rearrange("p o t d -> p (o t) d")

        block = ctx.enter_context(nc.Block())

        def rounds(eng, body):
            for g in range(4):
                body(g, g % 2)
            with eng.Fori(0, (NG - 6) // 2) as n:
                for u in range(2):
                    body(n * 2 + (4 + u), u)
            for g in range(NG - 2, NG + 1):
                body(g, g % 2)

        @block.sync
        def _(sp):
            def body(g, par):
                if inside(g + 2, NG):
                    sp.wait_ge(S["xlo_ready"], g + 1)
                    sp.dma_start(xT[:, par], one(xT_dram, g + 2)).then_inc(S["xT_loaded"][par], 32)
                if inside(g, NG):
                    wait_if(sp, S["out_ready"], (g - 1) * GT)
                    sp.dma_start(x2_in[:, par], one(x2_g, g)).then_inc(S["x2_loaded"][par], 32)
                if inside(g - 2, NG):
                    sp.wait_ge(S["out_ready"], (g - 1) * GT)
                    sp.dma_start(one(out_g, g - 2), out_sb[:, par]).then_inc(S["stored"][par], 32)

            for g in range(4):
                body(g, g % 2)
            with sp.Fori(0, (NG - 6) // 2) as n:
                for u in range(2):
                    body(n * 2 + (4 + u), u)
            for g in range(NG - 2, NG + 2):
                body(g, g % 2)
            for par in range(2):
                sp.wait_ge(S["stored"][par], through(NG - 2 + par, par, 16))

        @block.gpsimd
        def _(pool):
            def body(g, par):
                if inside(g, NG):
                    pool.wait_ge(S["idx_ready"], g + 1)
                    wait_if(pool, S["out_ready"], (g - 1) * GT)
                    hold(pool, S["held"])
                    for s in range(2):
                        for t in range(GT):
                            c = s * GT + t
                            pool.indirect_dma_start(
                                out=y_in[:, par, s, t], out_offset=None, in_=y_dram,
                                in_offset=bass.IndirectOffsetOnAxis(ap=rows_l[:, par, c:c + 1], axis=0)).then_inc(S["gathered"][par], 32)

            for par in range(2):
                pool.wait_ge(y_stored[par], through(NB - 2 + par, par, 16))
            rounds(pool, body)

        @block.scalar
        def _(act):
            def split_weights(m):
                act.copy(s_hi[:, m], s_raw[:, m]).then_inc(S["s_hi_ready"], 1)

            def split(g, par):
                act.wait_ge(S["xT_loaded"][par], through(g, par, 16))
                wait_if(act, S["up_ready"], (g - 1) * KH)
                act.copy(xT_h[:, par], xT[:, par]).then_inc(S["xhi_ready"], 1)

            split_weights(0)
            split(0, 0)
            split_weights(1)
            split_weights(2)

            def body(g, par):
                if not inside(g, NG):
                    return
                for b in range(KH):
                    act.wait_ge(S["gate_ready"], g * KH + (b + 1))
                    wait_if(act, S["hid_ready"], g * KH + (b - 1))
                    act.activation(gate[:, b % 2], ps_G[:, b % 2], ACT.Silu).then_inc(S["silu_ready"], 1)
                    act.wait_ge(S["hid_ready"], g * KH + (b + 1))
                    if b == 0:
                        wait_if(act, S["down_ready"], (g - 1) * 2)
                    act.copy(hidT_h[:, par, b], hidT[:, b % 2]).then_inc(S["hhi_ready"], 1)
                    if b == 1 and inside(g + 1, NG):
                        split(g + 1, 1 - par)

            rounds(act, body)

        @block.vector
        def _(dve):
            def split_weights(m):
                dve.wait_ge(S["s_hi_ready"], m + 1)
                dve.tensor_tensor(s_lo[:, m], s_raw[:, m], s_hi[:, m].bitcast(F32), ALU.subtract).then_inc(S["s_split"], 1)

            def split(g, par):
                dve.wait_ge(S["xhi_ready"], g + 1)
                wait_if(dve, S["up_ready"], (g - 1) * KH)
                dve.tensor_tensor(xT_l[:, par], xT[:, par], xT_h[:, par].bitcast(F32), ALU.subtract).then_inc(S["xlo_ready"], 1)

            split_weights(0)
            split(0, 0)
            split_weights(1)
            split_weights(2)
            ch = Chain(dve, S["weights"], 0)
            ch.step(dve.tensor_scalar(gap_sum[:], gap_exp[:], 1.0, None, ALU.add))
            ch.wait()
            ch.step(dve.reciprocal(gap_inv[:], gap_sum[:]))
            ch.wait()
            ch.step(dve.tensor_copy(weight_of[:, :, 0:GT], gap_inv[:]))
            ch.step(dve.tensor_tensor(weight_of[:, :, GT:2 * GT], gap_exp[:], gap_inv[:], ALU.mult))
            ch.wait()

            def tables(g, par):
                wait_if(dve, S["gathered"][par], through(g - 2, par, 16 * 2 * GT))
                wait_if(dve, S["out_ready"], (g - 1) * GT)
                r, w = (t[:, g] if isinstance(g, int) else t[:, bass.ds(g, 1)].rearrange("p o c -> p (o c)") for t in (row_of, weight_of))
                dve.tensor_copy(rows_l[:, par], r)
                dve.tensor_copy(weights_l[:, par], w).then_inc(S["idx_ready"], 1)

            def combine(g, par, h):
                ch = Chain(dve, S["c_comb"], g * GT + h * 2)
                if h == 0:
                    dve.wait_ge(S["x2_loaded"][par], through(g, par, 16))
                    wait_if(dve, S["stored"][par], through(g - 2, par, 16))
                    dve.wait_ge(S["gathered"][par], through(g, par, 16 * 2 * GT))
                    dve.wait_ge(S["idx_ready"], g + 1)
                ts = slice(2 * h, 2 * h + 2)
                dve.wait_ge(S["down_ready"], g * 2 + (h + 1))
                dve.scalar_tensor_tensor(out=out_sb[:, par, ts], in0=ps_D[:, h], scalar=-1.0, in1=x2_in[:, par, ts],
                                         op0=ALU.add, op1=ALU.add).then_inc(S["first_ready"], 1)
                dve.wait_ge(S["first_ready"], g * 2 + (h + 1))
                for t in range(2 * h, 2 * h + 2):
                    ch.step(dve.scalar_tensor_tensor(out=out_sb[:, par, t], in0=y_in[:, par, 0, t], scalar=weights_l[:, par, t:t + 1],
                                                     in1=out_sb[:, par, t], op0=ALU.mult, op1=ALU.add))
                ch.wait()
                for t in range(2 * h, 2 * h + 2):
                    dve.scalar_tensor_tensor(out=out_sb[:, par, t], in0=y_in[:, par, 1, t], scalar=weights_l[:, par, GT + t:GT + t + 1],
                                             in1=out_sb[:, par, t], op0=ALU.mult, op1=ALU.add).then_inc(S["out_ready"], 1)

            def body(g, par):
                if inside(g, NG):
                    tables(g, par)
                    for b in range(KH):
                        dve.wait_ge(S["silu_ready"], g * KH + (b + 1))
                        dve.wait_ge(S["up_ready"], g * KH + (b + 1))
                        dve.tensor_tensor(hidT[:, b % 2], ps_U[:, b % 2], gate[:, b % 2], ALU.mult).then_inc(S["hid_ready"], 1)
                        dve.wait_ge(S["hhi_ready"], g * KH + (b + 1))
                        dve.tensor_tensor(hidT_l[:, par, b], hidT[:, b % 2], hidT_h[:, par, b].bitcast(F32),
                                          ALU.subtract).then_inc(S["hlo_ready"], 1)
                        if b == 1 and inside(g + 1, NG):
                            split(g + 1, 1 - par)
                        if b == 1 and inside(g - 1, NG):
                            combine(g - 1, 1 - par, 0)
                elif inside(g - 1, NG):
                    combine(g - 1, 1 - par, 0)
                if inside(g - 1, NG):
                    combine(g - 1, 1 - par, 1)

            rounds(dve, body)

        @block.tensor
        def _(pe):
            def up_product(dst, m, par, b):
                n = 0
                for k in range(KD):
                    col = slice(k * H + b * P, k * H + (b + 1) * P)
                    for lhs, rhs in ((s_hi, xT_h), (s_lo, xT_h), (s_hi, xT_l)):
                        last = pe.matmul(dst, lhs[:, m, col], rhs[:, par, k], start=(n == 0), stop=(n == 3 * KD - 1))
                        n += 1
                return last

            def down(G, par, h):
                if h == 0:
                    pe.wait_ge(S["hlo_ready"], (G + 1) * KH)
                    if isinstance(G, int) and G == 0:
                        pe.wait_ge(S["s_split"], 3)
                wait_if(pe, S["first_ready"], (G - 1) * 2 + (h + 1))
                for t in range(2):
                    n = 0
                    for k in range(KH):
                        col = slice((2 * h + t) * P, (2 * h + t + 1) * P)
                        for lhs, rhs in ((hidT_h, s_hi), (hidT_l, s_hi), (hidT_h, s_lo)):
                            last = pe.matmul(ps_D[:, h, t], lhs[:, par, k, col], rhs[:, 2, k * D:(k + 1) * D],
                                             start=(n == 0), stop=(n == 3 * KH - 1))
                            n += 1
                last.then_inc(S["down_ready"], 1)

            def body(g, par):
                if inside(g, NG):
                    pe.wait_ge(S["xlo_ready"], g + 1)
                for b in range(KH):
                    if inside(g, NG):
                        wait_if(pe, S["silu_ready"], g * KH + (b - 1))
                        if isinstance(g, int) and g == 0 and b == 0:
                            pe.wait_ge(S["s_split"], 1)
                        up_product(ps_G[:, b % 2], 0, par, b).then_inc(S["gate_ready"], 1)
                        wait_if(pe, S["hid_ready"], g * KH + (b - 1))
                        if isinstance(g, int) and g == 0 and b == 0:
                            pe.wait_ge(S["s_split"], 2)
                        up_product(ps_U[:, b % 2], 1, par, b).then_inc(S["up_ready"], 1)
                    if b % 2 == 1 and inside(g - 1, NG):
                        down(g - 1, 1 - par, b // 2)

            rounds(pe, body)


def kernel(**inputs):
    import numpy as np
    import concourse.bacc as bacc
    from concourse.bass_utils import run_bass_kernel_spmd as run

    def arr(name):
        return np.asarray(inputs[name])

    x = arr("x")
    B, N, D = x.shape
    E, H, _ = arr("L0_ffn_w1").shape
    P_, KD, KH = 128, D // 128, H // 128

    def up_T(w):
        return w.reshape(H, KD, P_).transpose(2, 1, 0).reshape(P_, KD * H)

    def down_T(w):
        return w.reshape(D, KH, P_).transpose(2, 1, 0).reshape(P_, KH * D)

    w1, w2 = arr("L0_ffn_w1"), arr("L0_ffn_w2")
    arrays = {
        "in_x": x.reshape(B * N, D),
        "in_adj": arr("adj").reshape(B * N, N),
        "in_W": arr("L0_gnn_W"),
        "in_a": arr("L0_gnn_a"),
        "in_gate_wT": arr("L0_ffn_gate_w").reshape(E, KD, P_).transpose(2, 1, 0),
        "in_experts": np.stack([np.concatenate([up_T(w1[e]), down_T(w2[e])], axis=1) for e in range(E)], axis=1),
        "in_shared": np.concatenate([up_T(arr("L0_ffn_sg_gate")), up_T(arr("L0_ffn_sg_up")), down_T(arr("L0_ffn_sg_down"))], axis=1),
    }
    arrays = {n: np.ascontiguousarray(v) for n, v in arrays.items()}
    nc = bacc.Bacc("TRN2", target_bir_lowering=False, num_devices=1)
    aps = [nc.dram_tensor(n, v.shape, mybir.dt.from_np(v.dtype), kind="ExternalInput").ap() for n, v in arrays.items()]
    out = nc.dram_tensor("out_rows", [B * N, D], F32, kind="ExternalOutput").ap()
    gat_moe(nc, *aps, out)
    r = run(nc, [arrays], core_ids=[0])
    return np.asarray(r.results[0]["out_rows"]).reshape(B, N, D)
```
